# Optimizing a Trainium2 kernel written in Bass

```python
import numpy as np
import jax
import jax.numpy as jnp

def _softmax(x, axis=-1):
    return jax.nn.softmax(x, axis=axis)

def _gelu(x):
    return jax.nn.gelu(x, approximate=True)

def _silu(x):
    return jax.nn.silu(x)

def _sigmoid(x):
    return jax.nn.sigmoid(x)

def _layernorm(x, axis=-1, eps=1e-05):
    m = jnp.mean(x, axis=axis, keepdims=True)
    v = jnp.var(x, axis=axis, keepdims=True)
    return (x - m) / jnp.sqrt(v + eps)

def _scatter_add(tgt, idx, src, axis=0):
    return tgt.at[idx].add(src)

def _segment_sum(src, seg, n):
    return jax.ops.segment_sum(src, seg, n)
kernel_name = 'mk_recurrent_d1_jaxref_r4_e20291'

def setup_inputs(seed: int=0):
    np.random.seed(seed)
    _w = jnp.asarray

    def _L0_attn_setup():
        import jax, jax.numpy as jnp
        import numpy as np
        from jax import lax
        B, S, E, SD = (8, 1024, 256, 8)

        def _reference_tuple_inner(x, W_in, b_in, W_g, b_g, W_out, b_out):
            embed_dim = W_in.shape[0]
            combined = jnp.einsum('bse,ec->bsc', x, W_in) + b_in
            embed = combined[..., :embed_dim]
            state_in = combined[..., embed_dim:]
            gate = jax.nn.sigmoid(jnp.einsum('bsc,cd->bsd', combined, W_g) + b_g)

            def step(state, gs):
                g, si = gs
                new = g * state + (1.0 - g) * si
                return (new, new)
            state0 = jnp.zeros((x.shape[0], state_in.shape[-1]), dtype=x.dtype)
            g_t = jnp.moveaxis(gate, 1, 0)
            si_t = jnp.moveaxis(state_in, 1, 0)
            final_state, states = lax.scan(step, state0, (g_t, si_t))
            states = jnp.moveaxis(states, 0, 1)
            out = jnp.einsum('bsc,cd->bsd', jnp.concatenate([embed, states], axis=-1), W_out) + b_out
            return (out, final_state)
        key = jax.random.key(seed)
        ks = jax.random.split(key, 4)
        x = jax.random.normal(ks[0], (B, S, E), dtype=jnp.float32)
        W_in = jax.random.normal(ks[1], (E, E + SD), dtype=jnp.float32) / np.sqrt(E)
        b_in = jnp.zeros((E + SD,), dtype=jnp.float32)
        W_g = jax.random.normal(ks[2], (E + SD, SD), dtype=jnp.float32) / np.sqrt(E + SD)
        b_g = jnp.zeros((SD,), dtype=jnp.float32)
        W_out = jax.random.normal(ks[3], (E + SD, E), dtype=jnp.float32) / np.sqrt(E + SD)
        b_out = jnp.zeros((E,), dtype=jnp.float32)
        return {'x': x, 'W_in': W_in, 'b_in': b_in, 'W_g': W_g, 'b_g': b_g, 'W_out': W_out, 'b_out': b_out}
    _L0_attn_in = _L0_attn_setup()

    def _L0_ffn_setup():
        import jax, jax.numpy as jnp
        import numpy as np
        DIM = 256
        INTER = 256
        E = 32
        K = 4
        G = 8
        LG = 4
        ROUTE_SCALE = 1.0
        CAP_FACTOR = 1.25
        B, S = (4, 512)

        def _gate(xf, wg):
            logits = xf @ wg.T
            scores = jax.nn.softmax(logits, axis=-1)
            sg = scores.reshape(-1, G, E // G)
            group_scores = sg.max(axis=-1)
            _, gtop = jax.lax.top_k(group_scores, LG)
            keep_g = jnp.sum(jax.nn.one_hot(gtop, G, dtype=jnp.float32), axis=1) > 0
            masked = jnp.where(keep_g[:, :, None], sg, -jnp.inf).reshape(-1, E)
            _, idx = jax.lax.top_k(masked, K)
            w = jnp.take_along_axis(scores, idx, axis=1)
            w = w / (w.sum(-1, keepdims=True) + 1e-09) * ROUTE_SCALE
            return (w.astype(xf.dtype), idx)

        def _forward(x, wg, w1, w2, w3, sw1, sw2, sw3):
            shape = x.shape
            xf = x.reshape(-1, DIM)
            N = xf.shape[0]
            cap = max(1, int(CAP_FACTOR * N * K / E))
            w, idx = _gate(xf, wg)
            fe = idx.reshape(-1)
            oh = jax.nn.one_hot(fe, E, dtype=jnp.int32)
            pos = (jnp.cumsum(oh, axis=0) * oh).sum(-1) - 1
            keep = pos < cap
            dest = jnp.where(keep, fe * cap + pos, E * cap)
            tok = jnp.arange(N * K, dtype=jnp.int32) // K
            buf_tok = jnp.full((E * cap + 1,), N, jnp.int32).at[dest].set(tok)[:-1]
            buf_w = jnp.zeros((E * cap + 1,), x.dtype).at[dest].set(w.reshape(-1))[:-1]
            xp = jnp.concatenate([xf, jnp.zeros((1, DIM), x.dtype)], axis=0)
            xe = xp[buf_tok].reshape(E, cap, DIM)
            h = jax.nn.silu(jnp.einsum('ecd,edh->ech', xe, w1)) * jnp.einsum('ecd,edh->ech', xe, w3)
            out = jnp.einsum('ech,ehd->ecd', h, w2) * buf_w.reshape(E, cap, 1)
            y = jnp.zeros((N + 1, DIM), x.dtype).at[buf_tok].add(out.reshape(E * cap, DIM))[:N]
            z = jax.nn.silu(xf @ sw1) * (xf @ sw3) @ sw2
            return (y + z).reshape(shape)
        key = jax.random.key(seed)
        ks = jax.random.split(key, 9)
        sd = DIM ** (-0.5)
        si = INTER ** (-0.5)
        x = jax.random.normal(ks[0], (B, S, DIM), jnp.float32)
        wg = jax.random.normal(ks[1], (E, DIM), jnp.float32) * sd
        w1 = jax.random.normal(ks[2], (E, DIM, INTER), jnp.float32) * sd
        w3 = jax.random.normal(ks[3], (E, DIM, INTER), jnp.float32) * sd
        w2 = jax.random.normal(ks[4], (E, INTER, DIM), jnp.float32) * si
        sw1 = jax.random.normal(ks[5], (DIM, INTER), jnp.float32) * sd
        sw3 = jax.random.normal(ks[6], (DIM, INTER), jnp.float32) * sd
        sw2 = jax.random.normal(ks[7], (INTER, DIM), jnp.float32) * si
        return dict(x=x, wg=wg, w1=w1, w2=w2, w3=w3, sw1=sw1, sw2=sw2, sw3=sw3)
    _L0_ffn_in = _L0_ffn_setup()
    _d = {'L0_attn_x': _L0_attn_in['x'], 'L0_attn_W_in': _L0_attn_in['W_in'], 'L0_attn_b_in': _L0_attn_in['b_in'], 'L0_attn_W_g': _L0_attn_in['W_g'], 'L0_attn_b_g': _L0_attn_in['b_g'], 'L0_attn_W_out': _L0_attn_in['W_out'], 'L0_attn_b_out': _L0_attn_in['b_out'], 'L0_ffn_wg': _L0_ffn_in['wg'], 'L0_ffn_w1': _L0_ffn_in['w1'], 'L0_ffn_w2': _L0_ffn_in['w2'], 'L0_ffn_w3': _L0_ffn_in['w3'], 'L0_ffn_sw1': _L0_ffn_in['sw1'], 'L0_ffn_sw2': _L0_ffn_in['sw2'], 'L0_ffn_sw3': _L0_ffn_in['sw3']}
    _x0 = _d['L0_attn_x']
    _d['L0_attn_x'] = jax.random.normal(jax.random.fold_in(jax.random.key(seed), 1), (4, 2048, 256), dtype=_x0.dtype)
    del _x0
    return _d

def reference(L0_attn_x, L0_attn_W_in, L0_attn_b_in, L0_attn_W_g, L0_attn_b_g, L0_attn_W_out, L0_attn_b_out, L0_ffn_wg, L0_ffn_w1, L0_ffn_w2, L0_ffn_w3, L0_ffn_sw1, L0_ffn_sw2, L0_ffn_sw3):

    def _L0_attn_ref(x, W_in, b_in, W_g, b_g, W_out, b_out):
        import jax, jax.numpy as jnp
        import numpy as np
        from jax import lax
        B, S, E, SD = (8, 1024, 256, 8)

        def _reference_tuple_inner(x, W_in, b_in, W_g, b_g, W_out, b_out):
            embed_dim = W_in.shape[0]
            combined = jnp.einsum('bse,ec->bsc', x, W_in) + b_in
            embed = combined[..., :embed_dim]
            state_in = combined[..., embed_dim:]
            gate = jax.nn.sigmoid(jnp.einsum('bsc,cd->bsd', combined, W_g) + b_g)

            def step(state, gs):
                g, si = gs
                new = g * state + (1.0 - g) * si
                return (new, new)
            state0 = jnp.zeros((x.shape[0], state_in.shape[-1]), dtype=x.dtype)
            g_t = jnp.moveaxis(gate, 1, 0)
            si_t = jnp.moveaxis(state_in, 1, 0)
            final_state, states = lax.scan(step, state0, (g_t, si_t))
            states = jnp.moveaxis(states, 0, 1)
            out = jnp.einsum('bsc,cd->bsd', jnp.concatenate([embed, states], axis=-1), W_out) + b_out
            return (out, final_state)
        return _reference_tuple_inner(x, W_in, b_in, W_g, b_g, W_out, b_out)[0]

    def _L0_ffn_ref(x, wg, w1, w2, w3, sw1, sw2, sw3):
        import jax, jax.numpy as jnp
        import numpy as np
        DIM = 256
        INTER = 256
        E = 32
        K = 4
        G = 8
        LG = 4
        ROUTE_SCALE = 1.0
        CAP_FACTOR = 1.25
        B, S = (4, 512)

        def _gate(xf, wg):
            logits = xf @ wg.T
            scores = jax.nn.softmax(logits, axis=-1)
            sg = scores.reshape(-1, G, E // G)
            group_scores = sg.max(axis=-1)
            _, gtop = jax.lax.top_k(group_scores, LG)
            keep_g = jnp.sum(jax.nn.one_hot(gtop, G, dtype=jnp.float32), axis=1) > 0
            masked = jnp.where(keep_g[:, :, None], sg, -jnp.inf).reshape(-1, E)
            _, idx = jax.lax.top_k(masked, K)
            w = jnp.take_along_axis(scores, idx, axis=1)
            w = w / (w.sum(-1, keepdims=True) + 1e-09) * ROUTE_SCALE
            return (w.astype(xf.dtype), idx)

        def _forward(x, wg, w1, w2, w3, sw1, sw2, sw3):
            shape = x.shape
            xf = x.reshape(-1, DIM)
            N = xf.shape[0]
            cap = max(1, int(CAP_FACTOR * N * K / E))
            w, idx = _gate(xf, wg)
            fe = idx.reshape(-1)
            oh = jax.nn.one_hot(fe, E, dtype=jnp.int32)
            pos = (jnp.cumsum(oh, axis=0) * oh).sum(-1) - 1
            keep = pos < cap
            dest = jnp.where(keep, fe * cap + pos, E * cap)
            tok = jnp.arange(N * K, dtype=jnp.int32) // K
            buf_tok = jnp.full((E * cap + 1,), N, jnp.int32).at[dest].set(tok)[:-1]
            buf_w = jnp.zeros((E * cap + 1,), x.dtype).at[dest].set(w.reshape(-1))[:-1]
            xp = jnp.concatenate([xf, jnp.zeros((1, DIM), x.dtype)], axis=0)
            xe = xp[buf_tok].reshape(E, cap, DIM)
            h = jax.nn.silu(jnp.einsum('ecd,edh->ech', xe, w1)) * jnp.einsum('ecd,edh->ech', xe, w3)
            out = jnp.einsum('ech,ehd->ecd', h, w2) * buf_w.reshape(E, cap, 1)
            y = jnp.zeros((N + 1, DIM), x.dtype).at[buf_tok].add(out.reshape(E * cap, DIM))[:N]
            z = jax.nn.silu(xf @ sw1) * (xf @ sw3) @ sw2
            return (y + z).reshape(shape)
        return _forward(x, wg, w1, w2, w3, sw1, sw2, sw3)
    x = L0_attn_x
    xn = _layernorm(x, axis=-1)
    s = _L0_attn_ref(xn, L0_attn_W_in, L0_attn_b_in, L0_attn_W_g, L0_attn_b_g, L0_attn_W_out, L0_attn_b_out)
    g = _silu(_L0_ffn_ref(xn, L0_ffn_wg, L0_ffn_w1, L0_ffn_w2, L0_ffn_w3, L0_ffn_sw1, L0_ffn_sw2, L0_ffn_sw3))
    x = x + s * g
    return x

_drawn_inputs = setup_inputs


def setup_inputs(seed=0):
    import zlib

    import numpy as np

    out = dict(_drawn_inputs(seed))
    spreads = {'L0_attn_b_in': (0.0, 0.1), 'L0_attn_b_g': (0.0, 0.8), 'L0_attn_b_out': (0.0, 0.1)}
    factors = {'L0_attn_W_g': 3.169}
    for name, (base, spread) in spreads.items():
        noise = np.random.default_rng([zlib.crc32(name.encode()), seed]).standard_normal(out[name].shape)
        drawn = base * np.exp(spread * noise) if base else spread * noise
        out[name] = jnp.asarray(drawn.astype(out[name].dtype))
    for name, factor in factors.items():
        out[name] = (out[name] * factor).astype(out[name].dtype)
    return out
```

```python
import concourse.bass as bass
from concourse import mybir
from contextlib import ExitStack

F32 = mybir.dt.float32
F32R = mybir.dt.float32r
BF16 = mybir.dt.bfloat16
I32 = mybir.dt.int32
U32 = mybir.dt.uint32
ALU = mybir.AluOpType
ACT = mybir.ActivationFunctionType
X = mybir.AxisListType.X

P = 128
D = 256
KD = D // P
B, S = 4, 2048
N = B * S
TILES = N // P
GT = 4
GN = GT * P
GROUPS = N // GN
GROUPS_A_BATCH = S // GN
SD = 8
E = 32
EG = 8
KEEP_GROUPS = 4
K = 4
CAP = int(1.25 * N * K / E)
PAIR = 2 * P
PAIRS_MAX = CAP // PAIR
STRIDE = CAP + PAIR
ROW = D + 1 + E
TOK = D
WCOL = D + 1
FAR = 65536.0
LSC = D + E
SLOTS = 3
A_PAIRS = N // PAIR
EPS_LN = 1e-5
EPS_W = 1e-9
SCATTERS = 16 * GT * K
LN_STEPS = 9
ROUTE_STEPS = 32


def build(nc, x, w_in, b_in, w_g, b_g, w_out, b_out, wg, w1, w2, w3, sw1, sw2, sw3, out):
    ctx = ExitStack()
    with ctx:
        def sb(name, shape, dt=F32):
            return ctx.enter_context(nc.sbuf_tensor(name, shape, dt))

        def bank(name):
            return ctx.enter_context(nc.psum_tensor(name, [P, 512], F32))

        def sem(name):
            return ctx.enter_context(nc.semaphore(name))

        slot_rows = nc.dram_tensor("slot_rows", (E * STRIDE, ROW), F32).ap()
        y_dram = nc.dram_tensor("y_sum", (N, D), F32).ap()
        x_flat = x.rearrange("b s c -> (b s) c")
        out_flat = out.rearrange("b s c -> (b s) c")

        x_all = sb("x_all", [P, TILES, D])
        s_all = sb("s_all", [P, TILES, D])
        w_hl = [sb(f"w_hl{n}", [P, 6, KD, D], F32R) for n in range(2)]
        raw = sb("raw", [P, 3, KD * D])
        rows = [sb(f"rows{n}", [P, GT, ROW]) for n in range(SLOTS)]
        xh = sb("xh", [P, KD, GN], F32R)
        xl = sb("xl", [P, KD, GN], F32R)
        act = sb("act", [P, KD * PAIR])
        acth = sb("acth", [P, KD * PAIR], F32R)
        actl = sb("actl", [P, KD * PAIR], F32R)
        yw = sb("yw", [P, 2, D])
        wch = sb("wch", [P, KD, LSC], F32R)
        wcl = sb("wcl", [P, KD, LSC], F32R)
        wgh = sb("wgh", [P, KD, 40], F32R)
        wgl = sb("wgl", [P, KD, 40], F32R)
        wo = sb("wo", [P, D], F32R)
        state_hl = sb("state_hl", [P, GN], F32R)
        ident = sb("ident", [P, P])
        before = sb("before", [P, P], BF16)
        ones = sb("ones", [P, P], BF16)
        first_row = sb("first_row", [1, E], BF16)
        first_row_f = sb("first_row_f", [P, E])
        row_limit = sb("row_limit", [P, E])
        iota_f = sb("iota_f", [P, E])
        token = sb("token", [P, TILES])
        keep_state = sb("keep_state", [SD, GROUPS], U32)
        carry = sb("carry", [SD, 1])
        gate_bias = sb("gate_bias", [SD, 1])
        b_in_state = sb("b_in_state", [SD, 1])
        stats = sb("stats", [P, GT, 6])
        mean_var = sb("mean_var", [P, GT, 2])
        sd = sb("sd", [P, GT])
        rstd = sb("rstd", [P, GT])
        shift = sb("shift", [P, GT])
        logits = sb("logits", [P, GT, E])
        ex = sb("ex", [P, GT, E])
        masked = sb("masked", [P, GT, E])
        top = sb("top", [P, GT])
        total = sb("total", [P, GT])
        g_max = sb("g_max", [P, GT, EG])
        g_top = sb("g_top", [P, GT, 8])
        g_idx = sb("g_idx", [P, GT, 8], U32)
        g_hot = sb("g_hot", [P, GT, KEEP_GROUPS, EG])
        g_keep = sb("g_keep", [P, GT, EG])
        e_top = sb("e_top", [P, GT, 8])
        e_idx = sb("e_idx", [P, GT, 8], U32)
        hot = sb("hot", [P, GT, K, E])
        chosen = sb("chosen", [P, GT, E], BF16)
        sel = sb("sel", [P, GT, E])
        sel_sum = sb("sel_sum", [P, GT])
        dest = sb("dest", [P, GT, E])
        dest_idx = [sb(f"dest_idx{n}", [P, GT, K], U32) for n in range(SLOTS)]
        seen_new = sb("seen_new", [P, E])
        seen = sb("seen", [P, E], BF16)
        counts = sb("counts", [P, E])
        n_pairs_f = sb("n_pairs_f", [P, E])
        n_tmp = sb("n_tmp", [P, E])
        n_pairs = sb("n_pairs", [1, E], I32)
        n_rows = sb("n_rows", [1, E], I32)
        meta = sb("meta", [P, 4, 2, 1 + E])
        y_idx = sb("y_idx", [P, 2], U32)
        pad = sb("pad", [P, 1])
        primer = sb("primer", [2, 1])
        bias_low = sb("bias_low", [1, D], F32R)

        gate, omg, states = raw[0:SD, 0, :], raw[0:SD, 1, :], raw[0:SD, 2, :]
        zero_rows = rows[1][:, 0:2, :]
        row_in = rows[0]
        scratch = s_all[:, :, :].rearrange("p t c -> p (t c)")
        at = [0]

        def carve(parts, n):
            at[0] += n
            return scratch[0:parts, at[0] - n:at[0]]

        s_win = carve(P, KD * (D + SD)).rearrange("p (k c) -> p k c", k=KD)
        s_wout = carve(P, KD * D).rearrange("p (k c) -> p k c", k=KD)
        s_wout8 = carve(SD, D)
        s_wg = carve(P, KD * SD).rearrange("p (k c) -> p k c", k=KD)
        s_wg8 = carve(SD, SD)
        s_wr = carve(E, D)
        s_bin = carve(P, KD)
        s_bg = carve(SD, 1)
        s_bout = carve(1, D)
        s_wint = carve(P, KD * D).rearrange("p (k c) -> p k c", k=KD)
        s_wint8 = carve(SD, D)
        s_one = carve(1, 1)

        xt, pb = bank("xt"), bank("pb")
        h1, h3, yb, gb = bank("h1"), bank("h3"), bank("yb"), bank("gb")
        ls = [bank("ls0"), bank("ls1")]
        pos = pb[:, 0:GT * E].rearrange("p (t e) -> p t e", t=GT)
        cnt = pb[:, 0:E]

        x_loaded = [sem(f"x_loaded{n}") for n in range(SLOTS)]
        setup_loaded = sem("setup_loaded")
        small_loaded = sem("small_loaded")
        bias_moved = sem("bias_moved")
        consts_ready = sem("consts_ready")
        dve_consts = sem("dve_consts")
        setup_pe = sem("setup_pe")
        setup_act = sem("setup_act")
        setup_dve = sem("setup_dve")
        ln_step = sem("ln_step")
        var_ready = sem("var_ready")
        sd_ready = sem("sd_ready")
        norm_ready = sem("norm_ready")
        xn_ready = sem("xn_ready")
        xt_ready = sem("xt_ready")
        xh_ready = sem("xh_ready")
        xl_ready = sem("xl_ready")
        gb_ready = sem("gb_ready")
        tanh_ready = sem("tanh_ready")
        omg_ready = sem("omg_ready")
        gate_ready = sem("gate_ready")
        scan_step = sem("scan_step")
        states_ready = sem("states_ready")
        state_high = sem("state_high")
        state_high2 = sem("state_high2")
        state_low = sem("state_low")
        h1_ready = sem("h1_ready")
        h3_ready = sem("h3_ready")
        silu_ready = sem("silu_ready")
        act_ready = sem("act_ready")
        acth_ready = sem("acth_ready")
        actl_ready = sem("actl_ready")
        down_ready = sem("down_ready")
        z_ready = sem("z_ready")
        z_stored = sem("z_stored")
        ls_ready = sem("ls_ready")
        ls_taken = sem("ls_taken")
        route_step = sem("route_step")
        centred = sem("centred")
        exp_ready = sem("exp_ready")
        chosen_ready = sem("chosen_ready")
        pos_ready = sem("pos_ready")
        pos_taken = sem("pos_taken")
        seen_ready = sem("seen_ready")
        dispatch_ready = sem("dispatch_ready")
        scattered = [sem(f"scattered{n}") for n in range(SLOTS)]
        cnt_ready = sem("cnt_ready")
        count_step = sem("count_step")
        counts_ready = sem("counts_ready")
        zero_ready = sem("zero_ready")
        raw_loaded = sem("raw_loaded")
        wh_ready = sem("wh_ready")
        wl_ready = sem("wl_ready")
        zeros_stored = sem("zeros_stored")
        row_loaded = sem("row_loaded")
        meta_taken = sem("meta_taken")
        y_ready = sem("y_ready")
        added = [sem(f"added{n}") for n in range(2)]
        held = sem("held")
        sums_done = sem("sums_done")
        y_loaded = [sem(f"y_loaded{n}") for n in range(SLOTS)]
        silu_y = sem("silu_y")
        gated = sem("gated")
        out_ready = sem("out_ready")
        out_stored = [sem(f"out_stored{n}") for n in range(SLOTS)]

        block = ctx.enter_context(nc.Block())
        LOADS = 12

        def weight_view(w):
            return w.rearrange("(k p) n -> p k n", p=P)

        def raw_view(n):
            return raw[:, n, :].rearrange("p (k n) -> p k n", k=KD)

        def y_buf(c):
            return rows[c % SLOTS][:, :, :].rearrange("p t c -> p (t c)")[:, 0:GT * D] \
                .rearrange("p (t c) -> p t c", t=GT)

        def is_zero(v):
            return isinstance(v, int) and v <= 0

        def group_loop(eng, body):
            turns = (GROUPS - 1) // SLOTS
            for g in range(SLOTS):
                body(g, 0, g)
            with eng.Fori(1, turns) as i:
                for n in range(SLOTS):
                    body(i * SLOTS + n, i, n)
            for g in range(turns * SLOTS, GROUPS):
                body(g, g // SLOTS, g % SLOTS)

        def expert_loop(eng, section):
            section(0, 0, True)
            with eng.Fori(0, E // 2 - 1) as i:
                section(i * 2 + 1, 1, False)
                section(i * 2 + 2, 0, False)
            section(E - 1, 1, False)

        def pair_loop(eng, e, first, inner):
            n = eng.value_load(n_pairs[0:1, bass.ds(e, 1)], min_val=1, max_val=PAIRS_MAX)
            first()
            with eng.If(n > 1):
                with eng.Fori(1, n) as _:
                    inner()

        @block.sync
        def _(sp):
            def load_x(g):
                if g >= SLOTS:
                    sp.wait_ge(x_loaded[g % SLOTS], 16 * (g // SLOTS))
                sp.dma_start(x_all[:, GT * g:GT * g + GT, :],
                             x_flat[GN * g:GN * g + GN, :].rearrange("(t p) c -> p t c", p=P)
                             ).then_inc(x_loaded[g % SLOTS], 16)

            load_x(0)
            sp.dma_start(s_win, w_in.rearrange("(k p) c -> p k c", p=P)).then_inc(setup_loaded, 16)
            sp.dma_start(s_wout, w_out[0:D, :].rearrange("(k p) c -> p k c", p=P)).then_inc(setup_loaded, 16)
            sp.dma_start(s_wout8, w_out[D:D + SD, :]).then_inc(setup_loaded, 16)
            sp.dma_start(s_wr, wg).then_inc(setup_loaded, 16)
            for n, w in enumerate((sw1, sw3, sw2)):
                sp.dma_start(raw_view(n), weight_view(w)).then_inc(raw_loaded, 16)
            for g in range(1, GROUPS):
                load_x(g)
            sp.wait_ge(setup_dve, SETUP_DVE)
            sp.dma_start(wo[97:98, :].bitcast(F32), bias_low[:, :].bitcast(F32)).then_inc(bias_moved, 16)
            with sp.Fori(0, A_PAIRS) as q:
                sp.wait_ge(z_ready, 2 * q + 2)
                sp.dma_start(y_dram[bass.ds(q * PAIR, PAIR), :].rearrange("(t p) c -> p t c", p=P),
                             yw[:, :, :]).then_inc(z_stored, 16)

            def load_raw(e):
                for n, w in enumerate((w1, w3, w2)):
                    sp.dma_start(raw_view(n),
                                 w[bass.ds(e, 1), :, :].rearrange("a (k p) n -> p (a k) n", p=P)
                                 ).then_inc(raw_loaded, 16)

            def store_zeros(e):
                n = sp.value_load(n_rows[0:1, bass.ds(e, 1)], min_val=0, max_val=CAP)
                sp.dma_start(slot_rows[bass.ds(e * STRIDE + n, PAIR), :].rearrange("(t p) c -> p t c", p=P),
                             zero_rows).then_inc(zeros_stored, 16)

            sp.wait_ge(state_low, GROUPS)
            sp.wait_ge(state_high2, GROUPS)
            load_raw(0)
            sp.wait_ge(counts_ready, 1)
            sp.wait_ge(zero_ready, 1)
            store_zeros(0)
            for n in range(SLOTS):
                sp.wait_ge(scattered[n], SCATTERS * ((GROUPS - n + SLOTS - 1) // SLOTS))
            sp.wait_ge(zeros_stored, 16)
            pair = sp.alloc_register("sp_pair")
            sp.reg_mov(pair, 1)

            def copy_rows(e, j):
                sp.dma_start(row_in[:, 0:2, :],
                             slot_rows[bass.ds(e * STRIDE + j * PAIR, PAIR), :].rearrange("(t p) c -> p t c", p=P)
                             ).then_inc(row_loaded, 16)

            def load_rows(e, j):
                q = sp.snap(pair)
                sp.wait_ge(xt_ready, q + A_PAIRS)
                sp.wait_ge(meta_taken, q)
                copy_rows(e, j)
                sp.reg_add(pair, pair, 1)

            def section(e, following):
                n = sp.value_load(n_pairs[0:1, bass.ds(e, 1)], min_val=1, max_val=PAIRS_MAX)
                if following:
                    sp.wait_ge(wh_ready, e * 3 + 6)
                    sp.wait_ge(wl_ready, e * 3 + 6)
                    load_raw(e + 1)
                    store_zeros(e + 1)
                with sp.If(n > 1):
                    with sp.Fori(1, n) as j:
                        load_rows(e, j)
                if following:
                    sp.wait_ge(zeros_stored, e * 16 + 32)
                    load_rows(e + 1, 0)
                else:
                    load_rows(0, 0)

            copy_rows(0, 0)
            with sp.Fori(0, E - 1) as e:
                section(e, True)
            section(E - 1, False)
            q = sp.snap(pair)
            sp.wait_ge(xt_ready, q + A_PAIRS)
            sp.wait_ge(meta_taken, q)

            sp.wait_ge(sums_done, 1)
            for c in range(GROUPS):
                if c >= SLOTS:
                    sp.wait_ge(out_stored[c % SLOTS], 16 * (c // SLOTS))
                sp.dma_start(y_buf(c), y_dram[GN * c:GN * c + GN, :].rearrange("(t p) c -> p t c", p=P)
                             ).then_inc(y_loaded[c % SLOTS], 16)
            for n in range(SLOTS):
                sp.wait_ge(out_stored[n], 16 * ((GROUPS - n + SLOTS - 1) // SLOTS))

        @block.gpsimd
        def _(pool):
            pool.memset(ident[:, :], 0.0).then_inc(consts_ready, 1)
            pool.memset(before[:, :], 0.0).then_inc(consts_ready, 1)
            pool.memset(ones[:, :], 1.0).then_inc(consts_ready, 1)
            pool.iota(first_row_f[:, :], [[STRIDE, E]], 0, 0, allow_small_or_imprecise_dtypes=True).then_inc(consts_ready, 1)
            pool.iota(row_limit[:, :], [[STRIDE, E]], CAP, 0, allow_small_or_imprecise_dtypes=True).then_inc(consts_ready, 1)
            pool.iota(iota_f[:, :], [[1, E]], 0, 0, allow_small_or_imprecise_dtypes=True).then_inc(consts_ready, 1)
            pool.iota(token[:, :], [[P, TILES]], 0, 1, allow_small_or_imprecise_dtypes=True).then_inc(consts_ready, 1)
            pool.wait_ge(consts_ready, 7)
            pool.affine_select(out=ident[:, :], in_=ident[:, :], compare_op=ALU.not_equal, fill=1.0, base=0,
                               pattern=[[-1, P]], channel_multiplier=1).then_inc(consts_ready, 1)
            pool.affine_select(out=before[:, :], in_=before[:, :], compare_op=ALU.is_ge, fill=1.0, base=0,
                               pattern=[[-1, P]], channel_multiplier=1).then_inc(consts_ready, 1)
            pool.dma_start(s_wg, w_g[0:D, :].rearrange("(k p) c -> p k c", p=P)).then_inc(small_loaded, 16)
            pool.dma_start(s_wg8, w_g[D:D + SD, :]).then_inc(small_loaded, 16)
            pool.dma_start(s_bin, b_in[0:D].rearrange("(k p) -> p k", p=P),
                           allow_slow_non_contiguous=True).then_inc(small_loaded, 16)
            pool.dma_start(b_in_state[:, :], b_in[D:D + SD].rearrange("(p a) -> p a", a=1)).then_inc(small_loaded, 16)
            pool.dma_start(s_bg, b_g.rearrange("(p a) -> p a", a=1)).then_inc(small_loaded, 16)
            pool.dma_start(s_bout, b_out.rearrange("(a p) -> a p", a=1)).then_inc(small_loaded, 16)

            slot_bound = pool.to_reg(E * STRIDE - 1)
            token_bound = pool.to_reg(N - 1)

            def hold(sm, value):
                pool.wait_ge(sm, value)
                pool.sem_inc(held, 1)

            def scatter(g, turn, slot):
                hold(dispatch_ready, g + 1)
                for t in range(GT):
                    for k in range(K):
                        ins = pool.indirect_dma_start(
                            slot_rows, bass.IndirectOffsetOnAxis(dest_idx[slot][:, t, k:k + 1], 0),
                            rows[slot][:, t, :], None, bounds_check=slot_bound, oob_is_err=False)
                        ins.then_inc(scattered[slot], 16)

            group_loop(pool, scatter)

            for n in range(SLOTS):
                pool.wait_ge(scattered[n], SCATTERS * ((GROUPS - n + SLOTS - 1) // SLOTS))
            pool.memset(zero_rows, 0.0).then_inc(consts_ready, 1)
            pool.wait_ge(consts_ready, 10)
            pool.memset(rows[1][:, 0:2, TOK:TOK + 1], FAR).then_inc(zero_ready, 1)
            pool.wait_ge(z_stored, 16 * A_PAIRS)
            for t in range(2):
                pool.dma_start(primer[t:t + 1, :], wg[t:t + 1, 0:1]).then_inc(added[t], 16)
            pair = pool.alloc_register("pool_pair")
            pool.reg_mov(pair, 0)

            def add_pair(p):
                for t in range(2):
                    hold(y_ready, 2 * p + t + 3)
                    pool.indirect_dma_start(
                        y_dram, bass.IndirectOffsetOnAxis(y_idx[:, t:t + 1], 0), yw[:, t, :], None,
                        bounds_check=token_bound, oob_is_err=False, compute_op=ALU.add).then_inc(added[t], 16)
                pool.reg_add(pair, pair, 1)

            def section(e, slot, is_first):
                def first():
                    p = pool.snap(pair)
                    if not is_first:
                        for t in range(2):
                            pool.wait_ge(added[t], p * 16 + 16)
                    add_pair(p)
                pair_loop(pool, e, first, lambda: add_pair(pool.snap(pair)))

            pool.wait_ge(counts_ready, 1)
            expert_loop(pool, section)
            p = pool.snap(pair)
            for t in range(2):
                pool.wait_ge(added[t], p * 16 + 16)
            pool.sem_inc(sums_done, 1)
            for c in range(GROUPS):
                pool.wait_ge(out_ready, c + 1)
                pool.dma_start(out_flat[GN * c:GN * c + GN, :].rearrange("(t p) c -> p t c", p=P), y_buf(c)
                               ).then_inc(out_stored[c % SLOTS], 16)

        @block.tensor
        def _(pe):
            mm = nc.tensor.matmul
            pe.wait_ge(setup_loaded, 64)
            pe.wait_ge(small_loaded, 96)
            pe.wait_ge(consts_ready, 9)
            pe.wait_ge(dve_consts, DVE_CONSTS)
            for j in range(KD):
                for k in range(KD):
                    nc.tensor.transpose(xt[:, j * D + k * P:j * D + k * P + P], s_win[:, k, j * P:j * P + P], ident[:, :])
            for k in range(KD):
                nc.tensor.transpose(pb[0:SD, k * P:k * P + P], s_win[:, k, D:D + SD], ident[:, :])
            for k in range(KD):
                last = nc.tensor.transpose(h1[:, k * E:k * E + E], s_wr[:, k * P:k * P + P], ident[0:E, 0:E])
            last.then_inc(setup_pe, 1)
            pe.wait_ge(setup_act, 1)
            pe.wait_ge(setup_dve, 1)
            for m in range(KD):
                for j in range(KD):
                    mm(h3[:, m * D:m * D + D], s_wint[:, j, m * P:m * P + P], s_wout[:, j, :],
                       start=(j == 0), stop=(j == KD - 1))
            for m in range(KD):
                for j in range(KD):
                    mm(yb[:, m * SD:m * SD + SD], s_wint[:, j, m * P:m * P + P], s_wg[:, j, :], start=(j == 0), stop=False)
                mm(yb[:, m * SD:m * SD + SD], s_wint8[:, m * P:m * P + P], s_wg8, start=False, stop=True)
            for j in range(KD):
                mm(gb[0:SD, 0:1], s_wg[:, j, :], s_bin[:, j:j + 1], start=(j == 0), stop=False)
            mm(gb[0:SD, 0:1], s_wg8, b_in_state[:, :], start=False, stop=True)
            for j in range(KD):
                mm(ls[0][0:1, 0:D], s_bin[:, j:j + 1], s_wout[:, j, :], start=(j == 0), stop=False)
            mm(ls[0][0:1, 0:D], s_one, s_bout, start=False, stop=True).then_inc(setup_pe, 1)
            pe.wait_ge(setup_act, SETUP_ACT)
            pe.wait_ge(setup_dve, SETUP_DVE)
            pe.wait_ge(bias_moved, 16)
            pe.wait_ge(wh_ready, 3)
            pe.wait_ge(wl_ready, 3)

            def transposes(rows_t):
                for k in range(KD):
                    for t in range(2):
                        last = nc.tensor.transpose(xt[:, k * PAIR + t * P:k * PAIR + t * P + P],
                                                   rows_t[:, t, k * P:k * P + P], ident[:, :])
                last.then_inc(xt_ready, 1)

            def up(p, wts, c0):
                pe.wait_ge(xh_ready, p + 1)
                pe.wait_ge(xl_ready, p + 1)
                for n, (dst, taken, made) in enumerate(((h1, silu_ready, h1_ready), (h3, act_ready, h3_ready))):
                    if not is_zero(p):
                        pe.wait_ge(taken, p)
                    for m in range(KD):
                        for k in range(KD):
                            out = dst[:, m * PAIR:m * PAIR + PAIR]
                            high = wts[:, 2 * n, k, m * P:m * P + P]
                            low = wts[:, 2 * n + 1, k, m * P:m * P + P]
                            mm(out, high, xh[:, k, c0:c0 + PAIR], start=(k == 0), stop=False)
                            mm(out, low, xh[:, k, c0:c0 + PAIR], start=False, stop=False)
                            ins = mm(out, high, xl[:, k, c0:c0 + PAIR], start=False, stop=(k == KD - 1))
                    ins.then_inc(made, 1)

            def down(p, wts, taken):
                pe.wait_ge(acth_ready, p + 1)
                pe.wait_ge(actl_ready, p + 1)
                for sm, v in taken:
                    if not is_zero(v):
                        pe.wait_ge(sm, v)
                for t in range(2):
                    for k in range(KD):
                        c = k * PAIR + t * P
                        dst = yb[:, t * D:t * D + D]
                        mm(dst, acth[:, c:c + P], wts[:, 4, k, :], start=(k == 0), stop=False)
                        mm(dst, acth[:, c:c + P], wts[:, 5, k, :], start=False, stop=False)
                        ins = mm(dst, actl[:, c:c + P], wts[:, 4, k, :], start=False, stop=(k == KD - 1))
                ins.then_inc(down_ready, 1)

            def positions(g):
                pe.wait_ge(chosen_ready, g + 1)
                pe.wait_ge(seen_ready, g + 1)
                if not is_zero(g):
                    pe.wait_ge(pos_taken, g)
                for t in range(GT):
                    mm(pos[:, t, :], before[:, :], chosen[:, t, :], start=True, stop=False)
                    for u in range(t):
                        mm(pos[:, t, :], ones[:, :], chosen[:, u, :], start=False, stop=False)
                    mm(pos[:, t, :], ones[:, :], seen[:, :], start=False, stop=False)
                    ins = mm(pos[:, t, :], ones[0:1, :], first_row[:, :], start=False, stop=True)
                ins.then_inc(pos_ready, 1)

            def s_and_logits(g, t):
                n = g * GT + t
                dst = ls[t % 2]
                if not is_zero(n - 1):
                    pe.wait_ge(ls_taken, n - 1)
                cols = slice(t * P, t * P + P)
                for k in range(KD):
                    mm(dst[:, 0:LSC], xh[:, k, cols], wch[:, k, :], start=(k == 0), stop=False)
                    mm(dst[:, 0:LSC], xh[:, k, cols], wcl[:, k, :], start=False, stop=False)
                    mm(dst[:, 0:LSC], xl[:, k, cols], wch[:, k, :], start=False, stop=False)
                if t == 0:
                    pe.wait_ge(state_high2, g + 1)
                    pe.wait_ge(state_low, g + 1)
                mm(dst[:, 0:D], state_hl[:, cols], wo[:, :], start=False, stop=True).then_inc(ls_ready, 1)

            def group(g, turn, slot):
                pe.wait_ge(xn_ready, g * GT + GT)
                for i in range(2):
                    if not is_zero(g * 2 + i):
                        pe.wait_ge(xh_ready, g * 2 + i)
                        pe.wait_ge(xl_ready, g * 2 + i)
                    transposes(rows[slot][:, 2 * i:2 * i + 2, :])
                pe.wait_ge(xh_ready, g * 2 + 2)
                pe.wait_ge(xl_ready, g * 2 + 2)
                if not is_zero(g):
                    pe.wait_ge(tanh_ready, g)
                    pe.wait_ge(scan_step, g * 2)
                for k in range(KD):
                    mm(gb[0:40, :], wgh[:, k, :], xh[:, k, :], start=(k == 0), stop=False)
                    mm(gb[0:40, :], wgl[:, k, :], xh[:, k, :], start=False, stop=False)
                    ins = mm(gb[0:40, :], wgh[:, k, :], xl[:, k, :], start=False, stop=(k == KD - 1))
                ins.then_inc(gb_ready, 1)
                p = g * 2
                up(p, w_hl[1], 0)
                if not is_zero(g):
                    positions(g - 1)
                s_and_logits(g, 0)
                s_and_logits(g, 1)
                up(p + 1, w_hl[1], PAIR)
                down(p, w_hl[1], [(z_ready, 2 * p)])
                s_and_logits(g, 2)
                s_and_logits(g, 3)
                down(p + 1, w_hl[1], [(z_ready, 2 * p + 2)])

            group_loop(pe, group)
            positions(GROUPS - 1)
            pe.wait_ge(seen_ready, GROUPS + 1)
            mm(cnt, ones[:, :], seen[:, :], start=True, stop=True).then_inc(cnt_ready, 1)

            pair = pe.alloc_register("pe_pair")
            pe.reg_mov(pair, 0)

            def look_ahead(q):
                pe.wait_ge(row_loaded, q * 16 + 16)
                pe.wait_ge(xh_ready, q + A_PAIRS)
                pe.wait_ge(xl_ready, q + A_PAIRS)
                transposes(row_in)

            def down_before(q, wts):
                down(q + (A_PAIRS - 1), wts, [(y_ready, q * 2)])

            look_ahead(0)
            pe.wait_ge(z_ready, 2 * A_PAIRS)
            pe.wait_ge(counts_ready, 1)

            def section(e, slot, is_first):
                def one_pair(before_slot):
                    q = pe.snap(pair)
                    up(q + A_PAIRS, w_hl[slot], 0)
                    look_ahead(q + 1)
                    if before_slot is not None:
                        down_before(q, w_hl[before_slot])
                    pe.reg_add(pair, pair, 1)

                pe.wait_ge(wh_ready, e * 3 + 6)
                pe.wait_ge(wl_ready, e * 3 + 6)
                pair_loop(pe, e, lambda: one_pair(None if is_first else 1 - slot), lambda: one_pair(slot))

            expert_loop(pe, section)
            down_before(pe.snap(pair), w_hl[1])

        @block.scalar
        def _(sc):
            av = nc.scalar.activation
            n_setup = [0]

            def done(ins):
                n_setup[0] += 1
                ins.then_inc(setup_act, 1)

            sc.wait_ge(setup_pe, 1)
            done(av(s_wint, xt[:, :].rearrange("p (j c) -> p j c", j=KD), ACT.Copy))
            done(av(wch[:, :, D:LSC], h1[:, 0:KD * E].rearrange("p (k e) -> p k e", k=KD), ACT.Copy))
            sc.wait_ge(dve_consts, DVE_CONSTS)
            done(av(wgh[:, :, 32:40], s_win[:, :, D:D + SD], ACT.Copy))
            done(av(wo[0:SD, :], s_wout8, ACT.Copy))
            done(av(wo[32:32 + SD, :], s_wout8, ACT.Copy))
            sc.wait_ge(setup_pe, 2)
            done(av(wch[:, :, 0:D], h3[:, :].rearrange("p (k c) -> p k c", k=KD), ACT.Copy))
            done(av(wgh[:, :, 0:SD], yb[:, 0:KD * SD].rearrange("p (k c) -> p k c", k=KD), ACT.Copy))
            done(av(wo[96:97, :], ls[0][0:1, 0:D], ACT.Copy))

            def split_high(wts, loads):
                sc.wait_ge(raw_loaded, loads)
                for n in range(3):
                    av(wts[:, 2 * n, :, :], raw_view(n), ACT.Copy).then_inc(wh_ready, 1)

            split_high(w_hl[1], 48)
            assert n_setup[0] == SETUP_ACT

            def norm_sd(g):
                sc.wait_ge(var_ready, g + 1)
                av(sd[:, :], sd[:, :], ACT.Sqrt).then_inc(sd_ready, 1)

            def normalise(g, turn, slot):
                sc.wait_ge(norm_ready, g + 1)
                if not is_zero(turn):
                    sc.wait_ge(scattered[slot], turn * SCATTERS)
                for t in range(GT):
                    av(rows[slot][:, t, 0:D], x_all[:, bass.ds(g * GT + t, 1), :].rearrange("p a c -> p (a c)"),
                       ACT.Identity, bias=shift[:, t:t + 1], scale=rstd[:, t:t + 1]).then_inc(xn_ready, 1)

            def exps(g):
                sc.wait_ge(centred, g + 1)
                av(ex[:, :, :], ex[:, :, :], ACT.Exp).then_inc(exp_ready, 1)

            def take_ls(g, t):
                n = g * GT + t
                sc.wait_ge(ls_ready, n + 1)
                if t == 0 and not is_zero(g):
                    sc.wait_ge(centred, g)
                av(s_all[:, bass.ds(n, 1), :].rearrange("p a c -> p (a c)"), ls[t % 2][:, 0:D], ACT.Copy)
                av(logits[:, t, :], ls[t % 2][:, D:LSC], ACT.Copy).then_inc(ls_taken, 1)

            def xhigh(p, c0, wait=None):
                sc.wait_ge(xt_ready, p + 1)
                if wait is not None:
                    sc.wait_ge(*wait)
                av(xh[:, :, c0:c0 + PAIR], xt[:, :].rearrange("p (k t) -> p k t", k=KD), ACT.Copy).then_inc(xh_ready, 1)

            def silu(p):
                sc.wait_ge(h1_ready, p + 1)
                if not is_zero(p):
                    sc.wait_ge(actl_ready, p)
                av(act[:, :], h1[:, :], ACT.Silu).then_inc(silu_ready, 1)

            def act_high(p):
                sc.wait_ge(act_ready, p + 1)
                if not is_zero(p):
                    sc.wait_ge(down_ready, p)
                av(acth[:, :], act[:, :], ACT.Copy).then_inc(acth_ready, 1)

            def take_z(p):
                sc.wait_ge(down_ready, p + 1)
                if not is_zero(p):
                    sc.wait_ge(z_stored, 16 * p)
                for t in range(2):
                    av(yw[:, t, :], yb[:, t * D:t * D + D], ACT.Copy).then_inc(z_ready, 1)

            def gates(g):
                sc.wait_ge(gb_ready, g + 1)
                if is_zero(g):
                    sc.wait_ge(wl_ready, 3)
                else:
                    sc.wait_ge(state_low, g)
                    sc.wait_ge(state_high2, g)
                av(gate, gb[0:SD, :], ACT.Tanh, bias=gate_bias[:, :], scale=0.5).then_inc(tanh_ready, 1)
                sc.wait_ge(tanh_ready, g + 1)
                av(omg, gate, ACT.Copy, bias=0.5, scale=-0.5).then_inc(omg_ready, 1)
                sc.wait_ge(omg_ready, g + 1)
                av(gate, gate, ACT.Copy, bias=0.5, scale=0.5).then_inc(gate_ready, 1)
                sc.wait_ge(states_ready, g + 1)
                if not is_zero(g):
                    sc.wait_ge(ls_ready, g * GT)
                av(state_hl[0:SD, :], states, ACT.Copy).then_inc(state_high, 1)
                av(state_hl[64:64 + SD, :], states, ACT.Copy).then_inc(state_high2, 1)

            norm_sd(0)
            normalise(0, 0, 0)

            def group(g, turn, slot):
                p = g * 2
                for i in range(2):
                    xhigh(p + i, PAIR * i, None if is_zero(g) else (ls_ready, g * GT - 2 + 2 * i))
                if not is_zero(g):
                    exps(g - 1)
                gates(g)
                silu(p)
                act_high(p)
                take_ls(g, 0)
                take_ls(g, 1)
                silu(p + 1)
                take_z(p)
                act_high(p + 1)
                take_ls(g, 2)
                take_ls(g, 3)
                take_z(p + 1)
                if not (isinstance(g, int) and g == GROUPS - 1):
                    norm_sd(g + 1)
                    normalise(g + 1, turn + (slot + 1) // SLOTS, (slot + 1) % SLOTS)

            group_loop(sc, group)
            exps(GROUPS - 1)

            split_high(w_hl[0], 96)
            pair = sc.alloc_register("act_pair")
            sc.reg_mov(pair, 0)
            xhigh(A_PAIRS, 0, (h3_ready, A_PAIRS))
            sc.wait_ge(counts_ready, 1)

            def one_pair():
                p = sc.snap(pair) + A_PAIRS
                silu(p)
                xhigh(p + 1, 0, (h3_ready, p + 1))
                act_high(p)
                sc.reg_add(pair, pair, 1)

            def section(e, slot, is_first):
                def first():
                    p = sc.snap(pair) + A_PAIRS
                    one_pair()
                    if not (isinstance(e, int) and e == E - 1):
                        sc.wait_ge(down_ready, p)
                        split_high(w_hl[1 - slot], e * 48 + 144)
                pair_loop(sc, e, first, one_pair)

            expert_loop(sc, section)
            for c in range(GROUPS):
                sc.wait_ge(y_loaded[c % SLOTS], 16 * (c // SLOTS) + 16)
                av(y_buf(c), y_buf(c), ACT.Silu).then_inc(silu_y, 1)

        @block.vector
        def _(ve):
            v = nc.vector
            n_const = [0]

            def const(ins):
                n_const[0] += 1
                ins.then_inc(dve_consts, 1)

            const(v.memset(s_one, 1.0))
            const(v.memset(wo[:, :].bitcast(F32), 0.0))
            const(v.memset(wgh[:, :, :].bitcast(F32), 0.0))
            const(v.memset(wgl[:, :, :].bitcast(F32), 0.0))
            const(v.memset(state_hl[0:96, :].bitcast(F32), 0.0))
            const(v.memset(state_hl[96:P, :].bitcast(F32), 1.0))
            const(v.memset(keep_state[:, :].bitcast(I32), -1))
            ve.wait_ge(dve_consts, n_const[0])
            const(v.memset(keep_state[:, :].rearrange("p (b g) -> p b g", g=GROUPS_A_BATCH)[:, :, 0], 0))
            ve.wait_ge(consts_ready, 9)
            const(v.tensor_copy(first_row[:, :], first_row_f[0:1, :]))
            assert n_const[0] == DVE_CONSTS
            v.memset(seen[:, :], 0.0).then_inc(seen_ready, 1)

            n_setup = [0]

            def done(ins):
                n_setup[0] += 1
                ins.then_inc(setup_dve, 1)

            ve.wait_ge(setup_pe, 1)
            done(v.tensor_copy(s_wint8, pb[0:SD, 0:D]))
            ve.wait_ge(setup_act, 5)
            done(v.tensor_tensor(wcl[:, :, D:LSC], h1[:, 0:KD * E].rearrange("p (k e) -> p k e", k=KD),
                                 wch[:, :, D:LSC].bitcast(F32), ALU.subtract))
            done(v.tensor_tensor(wgl[:, :, 32:40], s_win[:, :, D:D + SD], wgh[:, :, 32:40].bitcast(F32), ALU.subtract))
            done(v.tensor_tensor(wo[64:64 + SD, :], s_wout8, wo[0:SD, :].bitcast(F32), ALU.subtract))
            ve.wait_ge(setup_pe, 2)
            done(v.tensor_scalar(gate_bias[:, :], gb[0:SD, 0:1], s_bg, 0.5, ALU.add, ALU.mult))
            ve.wait_ge(setup_act, 8)
            done(v.tensor_tensor(wcl[:, :, 0:D], h3[:, :].rearrange("p (k c) -> p k c", k=KD),
                                 wch[:, :, 0:D].bitcast(F32), ALU.subtract))
            done(v.tensor_tensor(wgl[:, :, 0:SD], yb[:, 0:KD * SD].rearrange("p (k c) -> p k c", k=KD),
                                 wgh[:, :, 0:SD].bitcast(F32), ALU.subtract))
            done(v.tensor_tensor(bias_low[:, :], ls[0][0:1, 0:D], wo[96:97, :].bitcast(F32), ALU.subtract))
            assert n_setup[0] == SETUP_DVE

            def split_low(wts, splits):
                ve.wait_ge(wh_ready, splits)
                for n in range(3):
                    v.tensor_tensor(wts[:, 2 * n + 1, :, :], raw_view(n), wts[:, 2 * n, :, :].bitcast(F32),
                                    ALU.subtract).then_inc(wl_ready, 1)

            split_low(w_hl[1], 3)

            def settled(sm, value):
                ve.wait_ge(sm, value)
                v.memset(pad[:, :], 0.0)

            def statistics(g, turn, slot):
                base = g * LN_STEPS
                ve.wait_ge(x_loaded[slot], turn * 16 + 16)
                for t in range(GT):
                    v.bn_stats(stats[:, t, :], x_all[:, bass.ds(g * GT + t, 1), :].rearrange("p a c -> p (a c)")
                               ).then_inc(ln_step, 1)
                settled(ln_step, base + GT)
                for t in range(GT):
                    v.bn_aggr(mean_var[:, t, :], stats[:, t, :]).then_inc(ln_step, 1)
                ve.wait_ge(ln_step, base + 8)
                v.tensor_scalar(sd[:, :], mean_var[:, :, 1], EPS_LN, None, ALU.add).then_inc(var_ready, 1)
                ve.wait_ge(sd_ready, g + 1)
                if not is_zero(g):
                    ve.wait_ge(xn_ready, g * GT)
                v.reciprocal(rstd[:, :], sd[:, :]).then_inc(ln_step, 1)
                ve.wait_ge(ln_step, base + 9)
                v.scalar_tensor_tensor(shift[:, :], mean_var[:, :, 0], -1.0, rstd[:, :], ALU.mult, ALU.mult
                                       ).then_inc(norm_ready, 1)

            def xlow(p, c0, wait=None):
                ve.wait_ge(xh_ready, p + 1)
                if wait is not None:
                    ve.wait_ge(*wait)
                v.tensor_tensor(xl[:, :, c0:c0 + PAIR], xt[:, :].rearrange("p (k t) -> p k t", k=KD),
                                xh[:, :, c0:c0 + PAIR].bitcast(F32), ALU.subtract).then_inc(xl_ready, 1)

            def gate_act(p):
                ve.wait_ge(h3_ready, p + 1)
                ve.wait_ge(silu_ready, p + 1)
                v.tensor_tensor(act[:, :], act[:, :], h3[:, :], ALU.mult).then_inc(act_ready, 1)

            def act_low(p):
                ve.wait_ge(acth_ready, p + 1)
                if not is_zero(p):
                    ve.wait_ge(down_ready, p)
                v.tensor_tensor(actl[:, :], act[:, :], acth[:, :].bitcast(F32), ALU.subtract).then_inc(actl_ready, 1)

            def recurrence(g):
                ve.wait_ge(gate_ready, g + 1)
                v.scalar_tensor_tensor(omg, gb[32:32 + SD, :], b_in_state[:, :], omg, ALU.add, ALU.mult
                                       ).then_inc(scan_step, 1)
                v.tensor_tensor(carry[:, :].bitcast(U32), states[:, GN - 1:GN].bitcast(U32),
                                keep_state[:, bass.ds(g, 1)], ALU.bitwise_and).then_inc(scan_step, 1)
                ve.wait_ge(scan_step, g * 2 + 2)
                v.tensor_tensor_scan(states, gate, omg, carry[:, :], ALU.mult, ALU.add).then_inc(states_ready, 1)
                ve.wait_ge(state_high, g + 1)
                v.tensor_tensor(state_hl[32:32 + SD, :], states, state_hl[0:SD, :].bitcast(F32), ALU.subtract
                                ).then_inc(state_low, 1)

            step = [0]

            def route_link(g, ins):
                step[0] += 1
                ins.then_inc(route_step, 1)
                ve.wait_ge(route_step, g * ROUTE_STEPS + step[0])

            def route_unlinked(g, ins):
                step[0] += 1
                ins.then_inc(route_step, 1)

            def over(ap, shape):
                return ap.to_broadcast(shape)

            def route_choose(g, slot):
                step[0] = 0
                ve.wait_ge(ls_taken, g * GT + GT)
                route_link(g, v.reduce_max(top[:, :], logits[:, :, :], X))
                v.tensor_tensor(ex[:, :, :], logits[:, :, :], over(top[:, :].unsqueeze(2), [P, GT, E]), ALU.subtract
                                ).then_inc(centred, 1)
                ve.wait_ge(exp_ready, g + 1)
                step[0] += 1
                v.reduce_max(g_max[:, :, :].rearrange("p t g -> p (t g)"),
                             ex[:, :, :].rearrange("p t (g e) -> p (t g) e", g=EG), X).then_inc(route_step, 1)
                ve.wait_ge(route_step, g * ROUTE_STEPS + step[0])
                v.reduce_sum(total[:, :], ex[:, :, :], X)
                for t in range(GT):
                    v.max(g_top[:, t, :], g_max[:, t, :]).then_inc(route_step, 1)
                step[0] += GT
                ve.wait_ge(route_step, g * ROUTE_STEPS + step[0])
                v.tensor_copy(rows[slot][:, :, TOK], token[:, bass.ds(g * GT, GT)])
                for t in range(GT):
                    v.max_index(g_idx[:, t, :], g_top[:, t, :], g_max[:, t, :]).then_inc(route_step, 1)
                step[0] += GT
                ve.wait_ge(route_step, g * ROUTE_STEPS + step[0])
                route_link(g, v.tensor_tensor(g_hot[:, :, :, :],
                                              over(iota_f[:, 0:EG].unsqueeze(1).unsqueeze(1), [P, GT, KEEP_GROUPS, EG]),
                                              over(g_idx[:, :, 0:KEEP_GROUPS].unsqueeze(3), [P, GT, KEEP_GROUPS, EG]),
                                              ALU.is_equal))
                route_link(g, v.reduce_sum(g_keep[:, :, :], g_hot[:, :, :, :].rearrange("p t k g -> p t g k"), X))
                route_link(g, v.tensor_scalar(g_keep[:, :, :], g_keep[:, :, :], 4.0, -4.0, ALU.mult, ALU.add))
                route_unlinked(g, v.tensor_tensor(masked[:, :, :].rearrange("p t (g e) -> p (t g) e", g=EG),
                                              ex[:, :, :].rearrange("p t (g e) -> p (t g) e", g=EG),
                                              over(g_keep[:, :, :].rearrange("p t g -> p (t g)").unsqueeze(2),
                                                   [P, GT * EG, E // EG]), ALU.add))
                settled(route_step, g * ROUTE_STEPS + step[0])
                for t in range(GT):
                    v.max(e_top[:, t, :], masked[:, t, :]).then_inc(route_step, 1)
                step[0] += GT
                settled(route_step, g * ROUTE_STEPS + step[0])
                for t in range(GT):
                    v.max_index(e_idx[:, t, :], e_top[:, t, :], masked[:, t, :]).then_inc(route_step, 1)
                step[0] += GT
                ve.wait_ge(route_step, g * ROUTE_STEPS + step[0])
                route_link(g, v.tensor_tensor(hot[:, :, :, :],
                                              over(iota_f[:, :].unsqueeze(1).unsqueeze(1), [P, GT, K, E]),
                                              over(e_idx[:, :, 0:K].unsqueeze(3), [P, GT, K, E]), ALU.is_equal))
                with nc.allow_low_precision(reason="zeros and ones"):
                    v.reduce_sum(chosen[:, :, :], hot[:, :, :, :].rearrange("p t k e -> p t e k"), X
                                 ).then_inc(chosen_ready, 1)
                ve.wait_ge(chosen_ready, g + 1)
                route_link(g, v.tensor_tensor(sel[:, :, :], ex[:, :, :], chosen[:, :, :], ALU.mult))
                route_link(g, v.reduce_sum(sel_sum[:, :], sel[:, :, :], X))
                route_link(g, v.scalar_tensor_tensor(sel_sum[:, :], total[:, :], EPS_W, sel_sum[:, :], ALU.mult, ALU.add))
                route_link(g, v.reciprocal(sel_sum[:, :], sel_sum[:, :]))
                v.tensor_tensor(rows[slot][:, :, WCOL:ROW], sel[:, :, :],
                                over(sel_sum[:, :].unsqueeze(2), [P, GT, E]), ALU.mult).then_inc(route_step, 1)
                step[0] += 1

            def route_place(g):
                ve.wait_ge(pos_ready, g + 1)
                route_link(g, v.tensor_tensor(dest[:, :, :], pos, over(row_limit[:, :].unsqueeze(1), [P, GT, E]),
                                              ALU.is_ge))
                v.scalar_tensor_tensor(dest[:, :, :], dest[:, :, :], FAR, pos, ALU.mult, ALU.add).then_inc(pos_taken, 1)
                ve.wait_ge(pos_taken, g + 1)
                route_link(g, v.tensor_tensor(hot[:, :, :, :], hot[:, :, :, :],
                                              over(dest[:, :, :].unsqueeze(2), [P, GT, K, E]), ALU.mult))
                v.reduce_sum(sel[:, :, 0:K], hot[:, :, :, :], X).then_inc(route_step, 1)
                with nc.allow_low_precision(reason="small whole numbers"):
                    v.reduce_sum(seen_new[:, :], chosen[:, :, :].rearrange("p t e -> p e t"), X).then_inc(route_step, 1)
                step[0] += 2
                ve.wait_ge(route_step, g * ROUTE_STEPS + step[0])

            def route_send(g, slot):
                v.tensor_copy(dest_idx[slot][:, :, :], sel[:, :, 0:K]).then_inc(dispatch_ready, 1)
                v.tensor_tensor(seen[:, :], seen[:, :], seen_new[:, :], ALU.add).then_inc(seen_ready, 1)
                assert step[0] == ROUTE_STEPS, step[0]

            statistics(0, 0, 0)

            def group(g, turn, slot):
                p = g * 2
                for i in range(2):
                    xlow(p + i, PAIR * i, None if is_zero(g) else (ls_ready, g * GT - 2 + 2 * i))
                before_slot = (slot - 1) % SLOTS
                if not is_zero(g):
                    route_choose(g - 1, before_slot)
                recurrence(g)
                gate_act(p)
                act_low(p)
                if not is_zero(g):
                    route_place(g - 1)
                gate_act(p + 1)
                if not is_zero(g):
                    route_send(g - 1, before_slot)
                act_low(p + 1)
                if not (isinstance(g, int) and g == GROUPS - 1):
                    statistics(g + 1, turn + (slot + 1) // SLOTS, (slot + 1) % SLOTS)

            group_loop(ve, group)
            last_slot = (GROUPS - 1) % SLOTS
            route_choose(GROUPS - 1, last_slot)
            route_place(GROUPS - 1)
            route_send(GROUPS - 1, last_slot)

            ve.wait_ge(cnt_ready, 1)
            steps = [0]

            def count_link(ins):
                steps[0] += 1
                ins.then_inc(count_step, 1)
                ve.wait_ge(count_step, steps[0])

            count_link(v.tensor_scalar(counts[:, :], cnt, float(CAP), None, ALU.min))
            count_link(v.tensor_scalar(n_pairs_f[:, :], counts[:, :], float(PAIR), 1.0, ALU.is_gt, ALU.add))
            for m in range(2, PAIRS_MAX):
                count_link(v.tensor_scalar(n_tmp[:, :], counts[:, :], float(PAIR * m), None, ALU.is_gt))
                count_link(v.tensor_tensor(n_pairs_f[:, :], n_pairs_f[:, :], n_tmp[:, :], ALU.add))
            count_link(v.tensor_copy(n_rows[:, :], counts[0:1, :]))
            v.tensor_copy(n_pairs[:, :], n_pairs_f[0:1, :]).then_inc(counts_ready, 1)

            split_low(w_hl[0], 6)
            pair = ve.alloc_register("dve_pair")
            ve.reg_mov(pair, 0)

            def take_meta(q):
                ve.wait_ge(row_loaded, q * 16 + 16)
                v.tensor_copy(meta[:, bass.ds(q % 4, 1), :, :].rearrange("p a t c -> p (a t) c"),
                              row_in[:, 0:2, TOK:ROW]).then_inc(meta_taken, 1)

            def take_y_before(q, e):
                ve.wait_ge(meta_taken, q)
                ve.wait_ge(down_ready, q + A_PAIRS)
                for t in range(2):
                    ve.wait_ge(added[t], q * 16)
                    m = meta[:, bass.ds((q + 3) % 4, 1), t, :].rearrange("p a c -> p (a c)")
                    v.tensor_copy(y_idx[:, t:t + 1], m[:, 0:1])
                    v.tensor_scalar(yw[:, t, :], yb[:, t * D:t * D + D], m[:, bass.ds(e + 1, 1)], None, ALU.mult
                                    ).then_inc(y_ready, 1)

            ve.wait_ge(z_stored, 16 * A_PAIRS)
            v.memset(pad[:, :], 0.0).then_inc(y_ready, 2)
            take_meta(0)
            xlow(A_PAIRS, 0, (h3_ready, A_PAIRS))
            ve.wait_ge(counts_ready, 1)

            def one_pair(e_before):
                q = ve.snap(pair)
                p = q + A_PAIRS
                take_meta(q + 1)
                gate_act(p)
                xlow(p + 1, 0, (h3_ready, p + 1))
                if e_before is not None:
                    take_y_before(q, e_before)
                act_low(p)
                ve.reg_add(pair, pair, 1)

            def section(e, slot, is_first):
                def first():
                    p = ve.snap(pair) + A_PAIRS
                    one_pair(None if is_first else e - 1)
                    if not (isinstance(e, int) and e == E - 1):
                        ve.wait_ge(down_ready, p)
                        split_low(w_hl[1 - slot], e * 3 + 9)
                pair_loop(ve, e, first, lambda: one_pair(e))

            expert_loop(ve, section)
            take_y_before(ve.snap(pair), E - 1)

            for c in range(GROUPS):
                ve.wait_ge(silu_y, c + 1)
                v.tensor_tensor(y_buf(c), y_buf(c), s_all[:, GT * c:GT * c + GT, :], ALU.mult).then_inc(gated, 1)
                ve.wait_ge(gated, c + 1)
                v.tensor_tensor(y_buf(c), y_buf(c), x_all[:, GT * c:GT * c + GT, :], ALU.add).then_inc(out_ready, 1)


SETUP_ACT = 8
SETUP_DVE = 8
DVE_CONSTS = 9

_INS = ["L0_attn_x", "L0_attn_W_in", "L0_attn_b_in", "L0_attn_W_g", "L0_attn_b_g", "L0_attn_W_out", "L0_attn_b_out",
        "L0_ffn_wg", "L0_ffn_w1", "L0_ffn_w2", "L0_ffn_w3", "L0_ffn_sw1", "L0_ffn_sw2", "L0_ffn_sw3"]


def kernel(**inputs):
    import numpy as np
    import concourse.bacc as bacc
    from concourse.bass_utils import run_bass_kernel_spmd

    nc = bacc.Bacc("TRN2", target_bir_lowering=False, num_devices=1)
    arrays, args = {}, []
    for name in _INS:
        a = np.ascontiguousarray(inputs[name])
        arrays[name] = a
        args.append(nc.dram_tensor(name, a.shape, mybir.dt.from_np(a.dtype), kind="ExternalInput").ap())
    out = nc.dram_tensor("out", (B, S, D), F32, kind="ExternalOutput").ap()
    build(nc, *args, out)
    r = run_bass_kernel_spmd(nc, [arrays], core_ids=[0])
    return r.results[0]["out"]
```

```python
import concourse.bass as bass
from concourse import mybir
from contextlib import ExitStack

F32 = mybir.dt.float32
F32R = mybir.dt.float32r
BF16 = mybir.dt.bfloat16
I32 = mybir.dt.int32
U32 = mybir.dt.uint32
ALU = mybir.AluOpType
ACT = mybir.ActivationFunctionType
X = mybir.AxisListType.X

P = 128
D = 256
KD = D // P
B, S = 4, 2048
N = B * S
TILES = N // P
GT = 4
GN = GT * P
GROUPS = N // GN
SD = 8
E = 32
EG = 8
KEEP_GROUPS = 4
K = 4
CAP = int(1.25 * N * K / E)
PAIR = 2 * P
PAIRS = CAP // PAIR - 1
STRIDE = CAP + PAIR
ROW = D + 1 + E
TOK = D
WCOL = D + 1
FAR = 65536.0
LSC = D + E
CHUNK = 2
CHUNKS = TILES // CHUNK
SLOTS = 4
Y_BUFS = 2 * SLOTS
A_PAIRS = N // PAIR
EPS_LN = 1e-5
EPS_W = 1e-9
MARKER = -8.0
MARK = 8.0
SCATTERS = 16 * GT * K
NORM_STEPS = 4
LEAD = SLOTS + 1
ROUTE_STEPS = 32


def build(nc, x, w_in, b_in, w_g, b_g, w_out, b_out, wg, w1, w2, w3, sw1, sw2, sw3, out):
    ctx = ExitStack()
    with ctx:
        def sb(name, shape, dt=F32):
            return ctx.enter_context(nc.sbuf_tensor(name, shape, dt))

        def bank(name):
            return ctx.enter_context(nc.psum_tensor(name, [P, 512], F32))

        def sem(name):
            return ctx.enter_context(nc.semaphore(name))

        slot_rows = nc.dram_tensor("slot_rows", (E * STRIDE, ROW), F32).ap()
        y_dram = nc.dram_tensor("y_sum", (N, D), F32).ap()
        x_flat = x.rearrange("b s c -> (b s) c")
        out_flat = out.rearrange("b s c -> (b s) c")

        x_all = sb("x_all", [P, TILES, D])
        s_all = sb("s_all", [P, TILES, D])
        w_hl = [sb(f"w_hl{n}", [P, 6, KD, D], F32R) for n in range(2)]
        raw = sb("raw", [P, 3, KD * D])
        rows = [sb(f"rows{n}", [P, GT, ROW]) for n in range(SLOTS)]
        xh = sb("xh", [P, KD, GN], F32R)
        xl = sb("xl", [P, KD, GN], F32R)
        act = sb("act", [P, KD * PAIR])
        acth = sb("acth", [P, KD * PAIR], F32R)
        actl = sb("actl", [P, KD * PAIR], F32R)
        yw = sb("yw", [P, 2, D])
        wch = sb("wch", [P, KD, LSC], F32R)
        wcl = sb("wcl", [P, KD, LSC], F32R)
        wgh = sb("wgh", [P, KD, 40], F32R)
        wgl = sb("wgl", [P, KD, 40], F32R)
        wo = sb("wo", [P, D], F32R)
        state_hl = sb("state_hl", [P, GN], F32R)
        ident = sb("ident", [P, P])
        before = sb("before", [P, P], BF16)
        ones = sb("ones", [P, P], BF16)
        first_row = sb("first_row", [1, E], BF16)
        first_row_f = sb("first_row_f", [P, E])
        row_limit = sb("row_limit", [P, E])
        iota_f = sb("iota_f", [P, E])
        token = sb("token", [P, TILES])
        gate_bias = sb("gate_bias", [SD, 1])
        b_in_state = sb("b_in_state", [SD, 1])
        stats = sb("stats", [P, GT, 6])
        mean_var = sb("mean_var", [P, SLOTS * GT, 2])
        sd = sb("sd", [P, SLOTS * GT])
        rstd = sb("rstd", [P, SLOTS * GT])
        shift = sb("shift", [P, SLOTS * GT])
        logits = sb("logits", [P, GT, E])
        ex = sb("ex", [P, GT, E])
        top = sb("top", [P, GT])
        total = sb("total", [P, GT])
        g_max = sb("g_max", [P, GT, EG + 4])
        g_top = sb("g_top", [P, GT, 12])
        g_marked = sb("g_marked", [P, GT, EG + 4])
        g_keep = sb("g_keep", [P, GT, EG])
        masked = sb("masked", [P, GT, E + 4])
        e_top = sb("e_top", [P, GT, 12])
        e_marked = sb("e_marked", [P, GT, E + 4])
        meta = sb("meta", [P, 4, 2, 1 + E])
        chosen = sb("chosen", [P, GT, E], BF16)
        sel_sum = sb("sel_sum", [P, GT])
        dest_top = sb("dest_top", [P, GT, 8])
        dest_idx = [sb(f"dest_idx{n}", [P, GT, K], U32) for n in range(SLOTS)]
        seen_new = sb("seen_new", [P, E])
        seen = sb("seen", [P, E], BF16)
        flags = sb("flags", [1, E], I32)
        n_zeros = sb("n_zeros", [1, E], I32)
        n_rows = sb("n_rows", [1, E], I32)
        y_idx = sb("y_idx", [P, 3, 2], U32)
        pad = sb("pad", [P, 1])
        warm = sb("warm", [1, 1])
        primer = sb("primer", [2, 1])

        gate, omg, states = raw[0:SD, 0, 0:PAIR], raw[0:SD, 1, 0:PAIR], raw[0:SD, 2, :]
        norm_scratch = [raw[:, 0, PAIR + n * SLOTS * GT:PAIR + (n + 1) * SLOTS * GT] for n in range(3)]
        sel = raw[:, 0, 2 * PAIR - GT * E:].rearrange("p (t e) -> p t e", t=GT)
        dest = raw[:, 1, PAIR:PAIR + GT * E].rearrange("p (t e) -> p t e", t=GT)
        counts, n_zeros_f, n_tmp = (logits[:, n, :] for n in range(3))
        has_fifth = seen_new[0:1, :].bitcast(I32)
        flags_f = logits[0:1, 3, :]
        zero_rows = rows[1][:, 0:2, :]
        row_in = [rows[0][:, 0:2, :], rows[0][:, 2:4, :], rows[2][:, 0:2, :]]
        y_out = [yw[:, :, :]] + [rows[3][:, :, :].rearrange("p t c -> p (t c)")[:, n * 2 * D:(n + 1) * 2 * D]
                                 .rearrange("p (t c) -> p t c", t=2) for n in range(2)]
        scratch = s_all[:, :, :].rearrange("p t c -> p (t c)")
        at = [0]

        def carve(parts, n):
            at[0] += n
            return scratch[0:parts, at[0] - n:at[0]]

        s_win = carve(P, KD * (D + SD)).rearrange("p (k c) -> p k c", k=KD)
        s_wout = carve(P, KD * D).rearrange("p (k c) -> p k c", k=KD)
        s_wout8 = carve(SD, D)
        s_wg = carve(P, KD * SD).rearrange("p (k c) -> p k c", k=KD)
        s_wg8 = carve(SD, SD)
        s_wr = carve(E, D)
        s_bin = carve(P, KD)
        s_bg = carve(SD, 1)
        s_bout = carve(1, D)
        s_wint = carve(P, KD * D).rearrange("p (k c) -> p k c", k=KD)
        s_wint8 = carve(SD, D)
        s_one = carve(1, 1)
        bias_low = carve(1, D)
        s_norm = [carve(P, SLOTS * GT) for _ in range(3)]

        xt, pb = bank("xt"), bank("pb")
        h1, h3, yb, gb = bank("h1"), bank("h3"), bank("yb"), bank("gb")
        ls = [bank("ls0"), bank("ls1")]
        pos = pb[:, 0:GT * E].rearrange("p (t e) -> p t e", t=GT)
        cnt = pb[:, 0:E]

        x_loaded = [sem(f"x_loaded{n}") for n in range(SLOTS)]
        setup_loaded = sem("setup_loaded")
        small_loaded = sem("small_loaded")
        bias_moved = sem("bias_moved")
        consts_ready = sem("consts_ready")
        dve_consts = sem("dve_consts")
        setup_pe = sem("setup_pe")
        setup_act = sem("setup_act")
        setup_dve = sem("setup_dve")
        stats_ready = sem("stats_ready")
        mean_ready = sem("mean_ready")
        norm_step = sem("norm_step")
        var_ready = sem("var_ready")
        sd_ready = sem("sd_ready")
        norm_ready = sem("norm_ready")
        xn_ready = sem("xn_ready")
        xt_ready = sem("xt_ready")
        xh_ready = sem("xh_ready")
        xl_ready = sem("xl_ready")
        gb_ready = sem("gb_ready")
        tanh_ready = sem("tanh_ready")
        omg_ready = sem("omg_ready")
        gate_ready = sem("gate_ready")
        gated_in = sem("gated_in")
        states_ready = sem("states_ready")
        state_high = sem("state_high")
        state_high2 = sem("state_high2")
        state_low = sem("state_low")
        h1_ready = sem("h1_ready")
        h3_ready = sem("h3_ready")
        silu_ready = sem("silu_ready")
        act_ready = sem("act_ready")
        acth_ready = sem("acth_ready")
        actl_ready = sem("actl_ready")
        down_ready = sem("down_ready")
        z_ready = sem("z_ready")
        z_stored = sem("z_stored")
        ls_ready = sem("ls_ready")
        ls_taken = sem("ls_taken")
        route_step = sem("route_step")
        centred = sem("centred")
        exp_ready = sem("exp_ready")
        chosen_ready = sem("chosen_ready")
        pos_ready = sem("pos_ready")
        pos_taken = sem("pos_taken")
        seen_ready = sem("seen_ready")
        dispatch_ready = sem("dispatch_ready")
        scattered = [sem(f"scattered{n}") for n in range(SLOTS)]
        cnt_ready = sem("cnt_ready")
        count_step = sem("count_step")
        counts_ready = sem("counts_ready")
        zero_ready = sem("zero_ready")
        raw_loaded = sem("raw_loaded")
        wh_ready = sem("wh_ready")
        wl_ready = sem("wl_ready")
        zeros_stored = sem("zeros_stored")
        row_loaded = [sem(f"row_loaded{n}") for n in range(3)]
        meta_taken = sem("meta_taken")
        y_ready = sem("y_ready")
        added = [sem(f"added{n}") for n in range(3)]
        held = sem("held")
        y_loaded = [sem(f"y_loaded{n}") for n in range(Y_BUFS)]
        silu_y = sem("silu_y")
        gated = sem("gated")
        out_ready = sem("out_ready")
        out_stored = [sem(f"out_stored{n}") for n in range(Y_BUFS)]

        block = ctx.enter_context(nc.Block())
        LOADS = 12

        def weight_view(w):
            return w.rearrange("(k p) n -> p k n", p=P)

        def raw_view(n):
            return raw[:, n, :].rearrange("p (k n) -> p k n", k=KD)

        def tail_tokens(c):
            return slice(CHUNK * P * c, CHUNK * P * (c + 1))

        def tail_tiles(c):
            return slice(CHUNK * c, CHUNK * (c + 1))

        def y_buf(c):
            half = c // SLOTS % 2
            return rows[c % SLOTS][:, :, :].rearrange("p t c -> p (t c)")[:, half * CHUNK * D:(half + 1) * CHUNK * D] \
                .rearrange("p (t c) -> p t c", t=CHUNK)

        def is_zero(v):
            return isinstance(v, int) and v <= 0

        def group_loop(eng, body):
            turns = GROUPS // SLOTS - 1
            body(0, 0, 0)
            with eng.Fori(0, turns) as i:
                for n in range(1, SLOTS + 1):
                    body(i * SLOTS + n, i + n // SLOTS, n % SLOTS)
            for n in range(1, SLOTS):
                body(turns * SLOTS + n, turns, n)

        def norm_chunk(turn, slot):
            return turn + slot // 2 + 1

        def norm_column(slot):
            return (slot + SLOTS // 2) % SLOTS * GT

        def tile_cols(a, t):
            return a[:, :].rearrange("p (k t c) -> p k t c", k=KD, t=2)[:, :, t, :]

        def is_last(g):
            return isinstance(g, int) and g == GROUPS - 1

        def region(i):
            return slice(i * PAIR, i * PAIR + PAIR)

        def expert_loop(eng, section):
            section(0, 0, True)
            with eng.Fori(0, E // 2 - 1) as i:
                section(i * 2 + 1, 1, False)
                section(i * 2 + 2, 0, False)
            section(E - 1, 1, False)

        def row_buffer(slot):
            return 2 if slot == PAIRS else slot % 2

        def row_fills(e, slot):
            return 2 * e + slot // 2 + 1 + slot % 2

        def y_buffer(slot):
            return 2 if slot == PAIRS else (slot + 1) % 2

        def y_uses(e, slot):
            return 2 * e + slot // 2 - (slot + 1) % 2

        class PairCounter:
            def __init__(self, eng, name):
                self.eng, self.pairs, self.fifths = eng, eng.alloc_register(name + "_pair"), \
                    eng.alloc_register(name + "_fifth")
                eng.reg_mov(self.pairs, 0)
                eng.reg_mov(self.fifths, 0)
                self.flags, self.flag = eng.alloc_register(name + "_flags"), eng.alloc_register(name + "_flag")

            def load_flags(self):
                low = self.eng.value_load(flags[0:1, 0:1], min_val=0, max_val=2 ** (E // 2) - 1)
                high = self.eng.value_load(flags[0:1, E // 2:E // 2 + 1], min_val=0, max_val=2 ** (E // 2) - 1)
                self.eng.reg_mov(self.flags, high)
                self.eng.reg_mul(self.flags, self.flags, 2 ** (E // 2))
                self.eng.reg_add(self.flags, self.flags, low)

            def next_flag(self):
                self.eng.reg_alu(self.flag, self.flags, 1, ALU.bitwise_and)
                self.eng.reg_alu(self.flags, self.flags, 1, ALU.logical_shift_right)
                return self.eng.snap(self.flag)

            def now(self):
                return self.eng.snap(self.pairs)

            def fifths_now(self):
                return self.eng.snap(self.fifths)

            def next(self, slot):
                self.eng.reg_add(self.pairs, self.pairs, 1)
                if slot == PAIRS:
                    self.eng.reg_add(self.fifths, self.fifths, 1)

        def slots(eng, count, body):
            for slot in range(PAIRS):
                body(slot)
            with eng.If(count.next_flag() > 0):
                body(PAIRS)

        @block.sync
        def _(sp):
            def load_x(g):
                if g >= SLOTS:
                    sp.wait_ge(x_loaded[g % SLOTS], 16 * (g // SLOTS))
                sp.dma_start(x_all[:, GT * g:GT * g + GT, :],
                             x_flat[GN * g:GN * g + GN, :].rearrange("(t p) c -> p t c", p=P)
                             ).then_inc(x_loaded[g % SLOTS], 16)

            load_x(0)
            sp.dma_start(s_win, w_in.rearrange("(k p) c -> p k c", p=P)).then_inc(setup_loaded, 16)
            sp.dma_start(s_wout, w_out[0:D, :].rearrange("(k p) c -> p k c", p=P)).then_inc(setup_loaded, 16)
            sp.dma_start(s_wout8, w_out[D:D + SD, :]).then_inc(setup_loaded, 16)
            sp.dma_start(s_wr, wg).then_inc(setup_loaded, 16)
            load_x(1)
            for n, w in enumerate((sw1, sw3, sw2)):
                sp.dma_start(raw_view(n), weight_view(w)).then_inc(raw_loaded, 16)
            for g in range(2, GROUPS):
                load_x(g)
            with sp.Fori(0, A_PAIRS) as q:
                sp.wait_ge(z_ready, 2 * q + 2)
                sp.dma_start(y_dram[bass.ds(q * PAIR, PAIR), :].rearrange("(t p) c -> p t c", p=P),
                             yw[:, :, :]).then_inc(z_stored, 16)

            def load_raw(e):
                for n, w in enumerate((w1, w3, w2)):
                    sp.dma_start(raw_view(n),
                                 w[bass.ds(e, 1), :, :].rearrange("a (k p) n -> p (a k) n", p=P)
                                 ).then_inc(raw_loaded, 16)

            zeros = sp.alloc_register("sp_zeros")
            sp.reg_mov(zeros, 0)

            def store_zeros(e):
                n = sp.value_load(n_rows[0:1, bass.ds(e, 1)], min_val=0, max_val=CAP)
                stores = sp.value_load(n_zeros[0:1, bass.ds(e, 1)], min_val=1, max_val=PAIRS)
                with sp.Fori(0, stores) as j:
                    row = nc.s_assert_within(e * STRIDE + n + j * PAIR, 0, E * STRIDE - PAIR,
                                             skip_runtime_bounds_check_because="the last store starts before the "
                                             "fifth pair, or there is one store, behind at most CAP rows")
                    sp.dma_start(slot_rows[bass.ds(row, PAIR), :].rearrange("(t p) c -> p t c", p=P),
                                 zero_rows).then_inc(zeros_stored, 16)
                    sp.reg_add(zeros, zeros, 16)

            sp.wait_ge(state_low, A_PAIRS)
            sp.wait_ge(state_high2, A_PAIRS)
            sp.wait_ge(dispatch_ready, GROUPS)
            load_raw(0)
            sp.wait_ge(counts_ready, 1)
            sp.wait_ge(zero_ready, 1)
            store_zeros(0)
            for n in range(SLOTS):
                sp.wait_ge(scattered[n], 16 + SCATTERS * (GROUPS // SLOTS))
            taken, transposed = sp.alloc_register("sp_taken"), sp.alloc_register("sp_transposed")
            sp.reg_mov(taken, 0)
            sp.reg_mov(transposed, A_PAIRS)

            def load_rows(e, j, buf, started=2, zeros_too=False):
                before_last, before_last_xt, stored = sp.snap(taken), sp.snap(transposed), sp.snap(zeros)
                if zeros_too:
                    sp.wait_ge(zeros_stored, stored)
                if started >= 2:
                    sp.wait_ge(xt_ready, before_last_xt)
                    sp.wait_ge(meta_taken, before_last)
                sp.dma_start(row_in[buf], slot_rows[bass.ds(e * STRIDE + j * PAIR, PAIR), :]
                             .rearrange("(t p) c -> p t c", p=P)).then_inc(row_loaded[buf], 16)
                if started:
                    sp.reg_add(taken, taken, 1)
                    sp.reg_add(transposed, transposed, 1)

            def section(e, first, last):
                fifth = sp.value_load(has_fifth[0:1, bass.ds(e, 1)], min_val=0, max_val=1)
                load_rows(e, 1, row_buffer(0), 1 if first else 2)
                if not last:
                    sp.wait_ge(wh_ready, e * 3 + 6)
                    sp.wait_ge(wl_ready, e * 3 + 6)
                    load_raw(e + 1)
                    store_zeros(e + 1)
                load_rows(e, 2, row_buffer(1))
                load_rows(e, 3, row_buffer(2))

                def next_first(slot):
                    if last:
                        load_rows(0, 0, row_buffer(slot))
                    else:
                        load_rows(e + 1, 0, row_buffer(slot), zeros_too=True)

                with sp.If(fifth > 0):
                    load_rows(e, 4, row_buffer(3))
                    next_first(4)
                with sp.If(fifth < 1):
                    next_first(3)

            load_rows(0, 0, 1, 0, zeros_too=True)
            section(0, True, False)
            with sp.Fori(1, E - 1) as e:
                section(e, False, False)
            section(E - 1, False, True)
            sp.reg_add(taken, taken, 1)
            sp.reg_add(transposed, transposed, 1)
            taken_all, transposed_all = sp.snap(taken), sp.snap(transposed)
            sp.wait_ge(xt_ready, transposed_all)
            sp.wait_ge(meta_taken, taken_all)

            for c in range(CHUNKS):
                sp.wait_ge(out_ready, c + 1)
                sp.dma_start(out_flat[tail_tokens(c), :].rearrange("(t p) c -> p t c", p=P), y_buf(c)
                             ).then_inc(out_stored[c % Y_BUFS], 16)
            for n in range(Y_BUFS):
                sp.wait_ge(out_stored[n], 16 * (CHUNKS // Y_BUFS))

        @block.gpsimd
        def _(pool):
            pool.memset(ident[:, :], 0.0).then_inc(consts_ready, 1)
            pool.memset(before[:, :], 0.0).then_inc(consts_ready, 1)
            pool.memset(ones[:, :], 1.0).then_inc(consts_ready, 1)
            pool.iota(first_row_f[:, :], [[STRIDE, E]], 0, 0, allow_small_or_imprecise_dtypes=True).then_inc(consts_ready, 1)
            pool.iota(row_limit[:, :], [[STRIDE, E]], CAP, 0, allow_small_or_imprecise_dtypes=True).then_inc(consts_ready, 1)
            pool.iota(iota_f[:, :], [[1, E]], 0, 0, allow_small_or_imprecise_dtypes=True).then_inc(consts_ready, 1)
            pool.iota(token[:, :], [[P, TILES]], 0, 1, allow_small_or_imprecise_dtypes=True).then_inc(consts_ready, 1)
            pool.wait_ge(consts_ready, 7)
            pool.affine_select(out=ident[:, :], in_=ident[:, :], compare_op=ALU.not_equal, fill=1.0, base=0,
                               pattern=[[-1, P]], channel_multiplier=1).then_inc(consts_ready, 1)
            pool.affine_select(out=before[:, :], in_=before[:, :], compare_op=ALU.is_ge, fill=1.0, base=0,
                               pattern=[[-1, P]], channel_multiplier=1).then_inc(consts_ready, 1)
            slot_bound = pool.to_reg(E * STRIDE - 1)
            token_bound = pool.to_reg(N - 1)

            def hold(sm, value):
                pool.wait_ge(sm, value)
                pool.sem_inc(held, 1)

            for n in range(SLOTS):
                pool.dma_start(primer[0:1, :], wg[n:n + 1, 0:1]).then_inc(scattered[n], 16)
                pool.wait_ge(scattered[n], 16)

            def scatter(g, turn, slot):
                hold(dispatch_ready, g + 1)
                for t in range(GT):
                    for k in range(K):
                        ins = pool.indirect_dma_start(
                            slot_rows, bass.IndirectOffsetOnAxis(dest_idx[slot][:, t, k:k + 1], 0),
                            rows[slot][:, t, :], None, bounds_check=slot_bound, oob_is_err=False)
                        ins.then_inc(scattered[slot], 16)

            group_loop(pool, scatter)

            pool.wait_ge(z_stored, 16 * A_PAIRS)
            pool.dma_start(primer[0:1, :], wg[0:1, 0:1]).then_inc(added[2], 16)
            count = PairCounter(pool, "pool")

            def add_pair(slot):
                p = count.now()
                buf = y_buffer(slot)
                for t in range(2):
                    hold(y_ready, 2 * p + t + 3)
                    pool.indirect_dma_start(
                        y_dram, bass.IndirectOffsetOnAxis(y_idx[:, buf, t:t + 1], 0), y_out[buf][:, t, :], None,
                        bounds_check=token_bound, oob_is_err=False, compute_op=ALU.add).then_inc(added[buf], 16)
                count.next(slot)

            def all_added(e):
                for slot in (0, 1):
                    pool.wait_ge(added[y_buffer(slot)], 32 * (y_uses(e, slot) + (slot == 0)))
                pool.wait_ge(added[2], 32 * count.fifths_now() + 16)

            def section(e, w_slot, is_first):
                def body(slot):
                    if not (is_first and slot == 0):
                        add_pair(slot)
                    if slot == 0 and not is_first:
                        all_added(e)
                slots(pool, count, body)

            pool.wait_ge(counts_ready, 1)
            count.load_flags()
            expert_loop(pool, section)
            add_pair(0)
            all_added(E)
            pool.sem_inc(held, 1)
            for c in range(CHUNKS):
                if c >= Y_BUFS:
                    pool.wait_ge(out_stored[c % Y_BUFS], 16 * (c // Y_BUFS))
                pool.dma_start(y_buf(c), y_dram[tail_tokens(c), :].rearrange("(t p) c -> p t c", p=P)
                               ).then_inc(y_loaded[c % Y_BUFS], 16)

        @block.tensor
        def _(pe):
            mm = nc.tensor.matmul
            pe.wait_ge(setup_loaded, 64)
            pe.wait_ge(small_loaded, 96)
            pe.wait_ge(consts_ready, 9)
            pe.wait_ge(dve_consts, DVE_CONSTS)
            for j in range(KD):
                for k in range(KD):
                    nc.tensor.transpose(xt[:, j * D + k * P:j * D + k * P + P], s_win[:, k, j * P:j * P + P], ident[:, :])
            for k in range(KD):
                nc.tensor.transpose(pb[0:SD, k * P:k * P + P], s_win[:, k, D:D + SD], ident[:, :])
            for k in range(KD):
                last = nc.tensor.transpose(h1[:, k * E:k * E + E], s_wr[:, k * P:k * P + P], ident[0:E, 0:E])
            last.then_inc(setup_pe, 1)
            pe.wait_ge(setup_act, 1)
            pe.wait_ge(setup_dve, 1)
            for m in range(KD):
                for j in range(KD):
                    mm(h3[:, m * D:m * D + D], s_wint[:, j, m * P:m * P + P], s_wout[:, j, :],
                       start=(j == 0), stop=(j == KD - 1))
            for m in range(KD):
                for j in range(KD):
                    mm(yb[:, m * SD:m * SD + SD], s_wint[:, j, m * P:m * P + P], s_wg[:, j, :], start=(j == 0), stop=False)
                mm(yb[:, m * SD:m * SD + SD], s_wint8[:, m * P:m * P + P], s_wg8, start=False, stop=True)
            for j in range(KD):
                mm(gb[0:SD, 0:1], s_wg[:, j, :], s_bin[:, j:j + 1], start=(j == 0), stop=False)
            mm(gb[0:SD, 0:1], s_wg8, b_in_state[:, :], start=False, stop=True)
            for j in range(KD):
                mm(ls[0][0:1, 0:D], s_bin[:, j:j + 1], s_wout[:, j, :], start=(j == 0), stop=False)
            mm(ls[0][0:1, 0:D], s_one, s_bout, start=False, stop=True).then_inc(setup_pe, 1)
            def transposes(rows_t):
                for k in range(KD):
                    for t in range(2):
                        last = nc.tensor.transpose(xt[:, k * PAIR + t * P:k * PAIR + t * P + P],
                                                   rows_t[:, t, k * P:k * P + P], ident[:, :])
                last.then_inc(xt_ready, 1)

            def up(p, wts, cols, between=None):
                pe.wait_ge(xh_ready, p + 1)
                pe.wait_ge(xl_ready, p + 1)
                for n, (dst, taken, made) in enumerate(((h1, silu_ready, h1_ready), (h3, act_ready, h3_ready))):
                    if not is_zero(p):
                        pe.wait_ge(taken, p)
                    for m in range(KD):
                        for k in range(KD):
                            out = dst[:, m * PAIR:m * PAIR + PAIR]
                            high = wts[:, 2 * n, k, m * P:m * P + P]
                            low = wts[:, 2 * n + 1, k, m * P:m * P + P]
                            mm(out, high, xh[:, k, cols], start=(k == 0), stop=False)
                            mm(out, low, xh[:, k, cols], start=False, stop=False)
                            ins = mm(out, high, xl[:, k, cols], start=False, stop=(k == KD - 1))
                    ins.then_inc(made, 1)
                    if n == 0 and between is not None:
                        between()

            def down(p, wts, taken):
                for sm, v in taken:
                    if not is_zero(v):
                        pe.wait_ge(sm, v)
                for t in range(2):
                    pe.wait_ge(acth_ready, 2 * p + t + 1)
                    pe.wait_ge(actl_ready, 2 * p + t + 1)
                    for k in range(KD):
                        c = k * PAIR + t * P
                        dst = yb[:, t * D:t * D + D]
                        mm(dst, acth[:, c:c + P], wts[:, 4, k, :], start=(k == 0), stop=False)
                        mm(dst, acth[:, c:c + P], wts[:, 5, k, :], start=False, stop=False)
                        ins = mm(dst, actl[:, c:c + P], wts[:, 4, k, :], start=False, stop=(k == KD - 1))
                ins.then_inc(down_ready, 1)

            def positions(g):
                pe.wait_ge(chosen_ready, g + 1)
                pe.wait_ge(seen_ready, g + 1)
                if not is_zero(g):
                    pe.wait_ge(pos_taken, g)
                for t in range(GT):
                    mm(pos[:, t, :], before[:, :], chosen[:, t, :], start=True, stop=False)
                    for u in range(t):
                        mm(pos[:, t, :], ones[:, :], chosen[:, u, :], start=False, stop=False)
                    mm(pos[:, t, :], ones[:, :], seen[:, :], start=False, stop=False)
                    ins = mm(pos[:, t, :], ones[0:1, :], first_row[:, :], start=False, stop=True)
                ins.then_inc(pos_ready, 1)

            def s_and_logits(p, i):
                for t in range(2):
                    dst = ls[t]
                    if not is_zero(p):
                        pe.wait_ge(ls_taken, 2 * p - 1 + t)
                    cols = slice(i * PAIR + t * P, i * PAIR + t * P + P)
                    for k in range(KD):
                        mm(dst[:, 0:LSC], xh[:, k, cols], wch[:, k, :], start=(k == 0), stop=False)
                        mm(dst[:, 0:LSC], xh[:, k, cols], wcl[:, k, :], start=False, stop=False)
                        mm(dst[:, 0:LSC], xl[:, k, cols], wch[:, k, :], start=False, stop=False)

            def add_states(p, i):
                pe.wait_ge(state_high2, p + 1)
                pe.wait_ge(state_low, p + 1)
                for t in range(2):
                    cols = slice(i * PAIR + t * P, i * PAIR + t * P + P)
                    mm(ls[t][:, 0:D], state_hl[:, cols], wo[:, :], start=False, stop=True).then_inc(ls_ready, 1)

            def transpose_tokens(p, i, slot):
                pe.wait_ge(xn_ready, 2 * p + 2)
                if not is_zero(p):
                    pe.wait_ge(xh_ready, p)
                    pe.wait_ge(xl_ready, p)
                transposes(rows[slot][:, 2 * i:2 * i + 2, :])

            def gate_inputs(p, i):
                pe.wait_ge(xh_ready, p + 1)
                pe.wait_ge(xl_ready, p + 1)
                if not is_zero(p):
                    pe.wait_ge(tanh_ready, p)
                    pe.wait_ge(gated_in, p)
                cols = region(i)
                for k in range(KD):
                    mm(gb[0:40, 0:PAIR], wgh[:, k, :], xh[:, k, cols], start=(k == 0), stop=False)
                    mm(gb[0:40, 0:PAIR], wgl[:, k, :], xh[:, k, cols], start=False, stop=False)
                    ins = mm(gb[0:40, 0:PAIR], wgh[:, k, :], xl[:, k, cols], start=False, stop=(k == KD - 1))
                ins.then_inc(gb_ready, 1)

            transpose_tokens(0, 0, 0)
            pe.wait_ge(setup_act, SETUP_ACT)
            pe.wait_ge(setup_dve, SETUP_DVE)
            gate_inputs(0, 0)
            s_and_logits(0, 0)
            pe.wait_ge(wh_ready, 3)
            pe.wait_ge(wl_ready, 3)

            def group(g, turn, slot):
                for i in range(2):
                    p = g * 2 + i
                    has_next = i == 0 or not is_last(g)
                    if has_next:
                        transpose_tokens(p + 1, 1 - i, (slot + i) % SLOTS)
                    if is_zero(p):
                        pe.wait_ge(bias_moved, 16)
                    add_states(p, i)
                    if i == 1 and not is_zero(g):
                        positions(g - 1)

                    def meanwhile():
                        if not is_zero(p):
                            down(p - 1, w_hl[1], [(z_ready, 2 * p - 2)])
                        if has_next:
                            gate_inputs(p + 1, 1 - i)

                    up(p, w_hl[1], region(i), meanwhile)
                    if has_next:
                        s_and_logits(p + 1, 1 - i)

            group_loop(pe, group)
            down(A_PAIRS - 1, w_hl[1], [(z_ready, 2 * A_PAIRS - 2)])
            positions(GROUPS - 1)
            pe.wait_ge(seen_ready, GROUPS + 1)
            mm(cnt, ones[:, :], seen[:, :], start=True, stop=True).then_inc(cnt_ready, 1)

            count = PairCounter(pe, "pe")

            def look_ahead(q, buf, fills):
                pe.wait_ge(row_loaded[buf], fills * 16)
                pe.wait_ge(xh_ready, q + A_PAIRS)
                pe.wait_ge(xl_ready, q + A_PAIRS)
                transposes(row_in[buf])

            def down_before(q, wts):
                down(q + (A_PAIRS - 1), wts, [(y_ready, q * 2)])

            look_ahead(0, 1, 1)
            pe.wait_ge(z_ready, 2 * A_PAIRS)
            pe.wait_ge(counts_ready, 1)
            count.load_flags()

            def section(e, w_slot, is_first):
                def body(slot):
                    q = count.now()
                    fills = count.fifths_now() + 1 if slot == PAIRS else row_fills(e, slot)
                    up(q + A_PAIRS, w_hl[w_slot], bass.ds((q % 2) * PAIR, PAIR),
                       lambda: look_ahead(q + 1, row_buffer(slot), fills))
                    if slot > 0:
                        down_before(q, w_hl[w_slot])
                    elif not is_first:
                        down_before(q, w_hl[1 - w_slot])
                    count.next(slot)

                pe.wait_ge(wh_ready, e * 3 + 6)
                pe.wait_ge(wl_ready, e * 3 + 6)
                slots(pe, count, body)

            expert_loop(pe, section)
            down_before(count.now(), w_hl[1])

        @block.scalar
        def _(sc):
            av = nc.scalar.activation
            n_setup = [0]

            def done(ins):
                n_setup[0] += 1
                ins.then_inc(setup_act, 1)

            sc.dma_start(s_wg, w_g[0:D, :].rearrange("(k p) c -> p k c", p=P)).then_inc(small_loaded, 16)
            sc.dma_start(s_wg8, w_g[D:D + SD, :]).then_inc(small_loaded, 16)
            sc.dma_start(s_bin, b_in[0:D].rearrange("(k p) -> p k", p=P),
                           allow_slow_non_contiguous=True).then_inc(small_loaded, 16)
            sc.dma_start(b_in_state[:, :], b_in[D:D + SD].rearrange("(p a) -> p a", a=1)).then_inc(small_loaded, 16)
            sc.dma_start(s_bg, b_g.rearrange("(p a) -> p a", a=1)).then_inc(small_loaded, 16)
            sc.dma_start(s_bout, b_out.rearrange("(a p) -> a p", a=1)).then_inc(small_loaded, 16)

            def norm_sd(chunk, cols=slice(None)):
                sc.wait_ge(var_ready, chunk + 1)
                av(sd[:, cols], sd[:, cols], ACT.Sqrt).then_inc(sd_ready, 1)

            def normalise(g, turn, slot, tiles):
                sc.wait_ge(norm_ready, norm_chunk(turn, slot))
                if not is_zero(turn):
                    sc.wait_ge(scattered[slot], turn * SCATTERS + 16)
                for t in tiles:
                    c = norm_column(slot) + t
                    av(rows[slot][:, t, 0:D], x_all[:, bass.ds(g * GT + t, 1), :].rearrange("p a c -> p (a c)"),
                       ACT.Identity, bias=shift[:, c:c + 1], scale=rstd[:, c:c + 1]).then_inc(xn_ready, 1)

            sc.wait_ge(setup_pe, 1)
            done(av(s_wint, xt[:, :].rearrange("p (j c) -> p j c", j=KD), ACT.Copy))
            done(av(wch[:, :, D:LSC], h1[:, 0:KD * E].rearrange("p (k e) -> p k e", k=KD), ACT.Copy))
            sc.wait_ge(dve_consts, DVE_CONSTS)
            done(av(wgh[:, :, 32:40], s_win[:, :, D:D + SD], ACT.Copy))
            done(av(wo[0:SD, :], s_wout8, ACT.Copy))
            done(av(wo[32:32 + SD, :], s_wout8, ACT.Copy))
            norm_sd(0, slice(norm_column(0), None))
            normalise(0, 0, 0, range(GT))
            sc.wait_ge(setup_pe, 2)
            done(av(wch[:, :, 0:D], h3[:, :].rearrange("p (k c) -> p k c", k=KD), ACT.Copy))
            done(av(wgh[:, :, 0:SD], yb[:, 0:KD * SD].rearrange("p (k c) -> p k c", k=KD), ACT.Copy))
            done(av(wo[96:97, :], ls[0][0:1, 0:D], ACT.Copy))

            def split_high(wts, loads, matrices=range(3)):
                sc.wait_ge(raw_loaded, loads)
                for n in matrices:
                    av(wts[:, 2 * n, :, :], raw_view(n), ACT.Copy).then_inc(wh_ready, 1)

            assert n_setup[0] == SETUP_ACT

            def exps(g):
                sc.wait_ge(centred, g + 1)
                av(ex[:, :, :], ex[:, :, :], ACT.Exp).then_inc(exp_ready, 1)

            def take_ls(p, i, g):
                for t in range(2):
                    n = 2 * p + t
                    sc.wait_ge(ls_ready, n + 1)
                    if i == 0 and t == 0 and not is_zero(g):
                        sc.wait_ge(centred, g)
                    av(s_all[:, bass.ds(n, 1), :].rearrange("p a c -> p (a c)"), ls[t][:, 0:D], ACT.Copy)
                    av(logits[:, 2 * i + t, :], ls[t][:, D:LSC], ACT.Copy).then_inc(ls_taken, 1)

            def xhigh(p, cols, wait=None):
                sc.wait_ge(xt_ready, p + 1)
                if wait is not None:
                    sc.wait_ge(*wait)
                av(xh[:, :, cols], xt[:, :].rearrange("p (k t) -> p k t", k=KD), ACT.Copy).then_inc(xh_ready, 1)

            def silu(p):
                sc.wait_ge(h1_ready, p + 1)
                if not is_zero(p):
                    sc.wait_ge(actl_ready, 2 * p)
                av(act[:, :], h1[:, :], ACT.Silu).then_inc(silu_ready, 1)

            def act_high(p):
                sc.wait_ge(act_ready, p + 1)
                if not is_zero(p):
                    sc.wait_ge(down_ready, p)
                for t in range(2):
                    av(tile_cols(acth, t), tile_cols(act, t), ACT.Copy).then_inc(acth_ready, 1)

            def take_z(p):
                sc.wait_ge(down_ready, p + 1)
                if not is_zero(p):
                    sc.wait_ge(z_stored, 16 * p)
                for t in range(2):
                    av(yw[:, t, :], yb[:, t * D:t * D + D], ACT.Copy).then_inc(z_ready, 1)

            def gates(p):
                sc.wait_ge(gb_ready, p + 1)
                if is_zero(p):
                    sc.wait_ge(wl_ready, 3)
                else:
                    sc.wait_ge(states_ready, p)
                av(gate, gb[0:SD, 0:PAIR], ACT.Tanh, bias=gate_bias[:, :], scale=0.5).then_inc(tanh_ready, 1)
                sc.wait_ge(tanh_ready, p + 1)
                av(omg, gate, ACT.Copy, bias=0.5, scale=-0.5).then_inc(omg_ready, 1)
                sc.wait_ge(omg_ready, p + 1)
                av(gate, gate, ACT.Copy, bias=0.5, scale=0.5).then_inc(gate_ready, 1)

            def states_high(p, i):
                sc.wait_ge(states_ready, p + 1)
                if not is_zero(p - 1):
                    sc.wait_ge(ls_ready, 2 * p - 2)
                av(state_hl[0:SD, region(i)], states[:, region(i)], ACT.Copy).then_inc(state_high, 1)
                av(state_hl[64:64 + SD, region(i)], states[:, region(i)], ACT.Copy).then_inc(state_high2, 1)

            xhigh(0, region(0))
            split_high(w_hl[1], 48)
            sc.wait_ge(setup_dve, SETUP_DVE)
            sc.dma_start(wo[97:98, :].bitcast(F32), bias_low).then_inc(bias_moved, 16)
            gates(0)
            states_high(0, 0)

            def group(g, turn, slot):
                for i in range(2):
                    p = g * 2 + i
                    has_next = i == 0 or not is_last(g)
                    if i == 0 and not is_zero(g):
                        exps(g - 1)
                    if has_next:
                        xhigh(p + 1, region(1 - i), None if is_zero(p) else (h3_ready, p))
                    take_ls(p, i, g)
                    silu(p)
                    if i == 1:
                        take_z(p - 1)
                    if has_next:
                        gates(p + 1)
                    if not is_last(g):
                        normalise(g + 1, turn + (slot + 1) // SLOTS, (slot + 1) % SLOTS, range(2 * i, 2 * i + 2))
                    if i == 0 and not is_zero(g):
                        take_z(p - 1)
                    if has_next:
                        states_high(p + 1, 1 - i)
                    act_high(p)
                    if i == 1 and slot == 0:
                        norm_sd(turn + 1)

            group_loop(sc, group)
            exps(GROUPS - 1)
            take_z(A_PAIRS - 1)

            split_high(w_hl[0], 96)
            av(warm[:, :], iota_f[0:1, 0:1], ACT.Silu)
            count = PairCounter(sc, "act")
            xhigh(A_PAIRS, region(0), (h3_ready, A_PAIRS - 1))
            sc.wait_ge(counts_ready, 1)
            count.load_flags()

            def section(e, w_slot, is_first):
                def body(slot):
                    q = count.now()
                    p = q + A_PAIRS
                    silu(p)
                    xhigh(p + 1, bass.ds(((q + 1) % 2) * PAIR, PAIR), (h3_ready, p))
                    act_high(p)
                    if slot < 3 and not (isinstance(e, int) and e == E - 1):
                        if slot == 0:
                            sc.wait_ge(down_ready, p)
                        split_high(w_hl[1 - w_slot], e * 48 + 144, (slot,))
                    count.next(slot)
                slots(sc, count, body)

            expert_loop(sc, section)
            for c in range(CHUNKS):
                sc.wait_ge(y_loaded[c % Y_BUFS], 16 * (c // Y_BUFS) + 16)
                av(y_buf(c), y_buf(c), ACT.Silu).then_inc(silu_y, 1)

        @block.vector
        def _(ve):
            v = nc.vector
            n_const = [0]

            def const(ins):
                n_const[0] += 1
                ins.then_inc(dve_consts, 1)

            const(v.memset(s_one, 1.0))
            const(v.memset(wo[:, :].bitcast(F32), 0.0))
            for values, n in ((g_max, EG), (g_top, 8), (masked, E), (e_top, 8)):
                const(v.memset(values[:, :, n:n + 4], MARKER))
            const(v.memset(wgh[:, :, :].bitcast(F32), 0.0))
            const(v.memset(wgl[:, :, :].bitcast(F32), 0.0))
            const(v.memset(state_hl[0:96, :].bitcast(F32), 0.0))
            const(v.memset(state_hl[96:P, :].bitcast(F32), 1.0))
            ve.wait_ge(consts_ready, 9)
            const(v.tensor_copy(first_row[:, :], first_row_f[0:1, :]))
            assert n_const[0] == DVE_CONSTS
            v.memset(seen[:, :], 0.0).then_inc(seen_ready, 1)

            def settled(sm, value):
                ve.wait_ge(sm, value)
                v.memset(pad[:, :], 0.0)

            def statistics(g, turn, slot):
                ve.wait_ge(x_loaded[slot], turn * 16 + 16)
                if not is_zero(g):
                    ve.wait_ge(mean_ready, g * GT)
                for t in range(GT):
                    tile = g * GT + t
                    if not isinstance(g, int):
                        tile = nc.s_assert_within(tile, 0, TILES - 1, skip_runtime_bounds_check_because=
                                                  "the last turn skips the groups behind the last one")
                    v.bn_stats(stats[:, t, :], x_all[:, bass.ds(tile, 1), :].rearrange("p a c -> p (a c)")
                               ).then_inc(stats_ready, 1)
                settled(stats_ready, g * GT + GT)
                for t in range(GT):
                    v.bn_aggr(mean_var[:, norm_column(slot) + t, :], stats[:, t, :]).then_inc(mean_ready, 1)

            def variances(groups, cols=slice(None)):
                ve.wait_ge(mean_ready, groups * GT)
                v.tensor_scalar(sd[:, cols], mean_var[:, cols, 1], EPS_LN, None, ALU.add).then_inc(var_ready, 1)

            def scale_and_shift(chunk, groups, cols=slice(None), scratch=None):
                done = [chunk * NORM_STEPS]
                half_var, rstd0, newton = scratch or norm_scratch

                def link(ins):
                    done[0] += 1
                    ins.then_inc(norm_step, 1)
                    ve.wait_ge(norm_step, done[0])

                ve.wait_ge(sd_ready, chunk + 1)
                v.tensor_scalar(half_var[:, cols], mean_var[:, cols, 1], -0.5, -0.5 * EPS_LN, ALU.mult, ALU.add)
                link(v.reciprocal(rstd0[:, cols], sd[:, cols]))
                link(v.tensor_tensor(newton[:, cols], rstd0[:, cols], rstd0[:, cols], ALU.mult))
                link(v.tensor_tensor(newton[:, cols], newton[:, cols], half_var[:, cols], ALU.mult))
                if not is_zero(groups):
                    ve.wait_ge(xn_ready, groups * GT)
                link(v.scalar_tensor_tensor(rstd[:, cols], newton[:, cols], 1.5, rstd0[:, cols], ALU.add, ALU.mult))
                v.scalar_tensor_tensor(shift[:, cols], mean_var[:, cols, 0], -1.0, rstd[:, cols], ALU.mult, ALU.mult
                                       ).then_inc(norm_ready, 1)

            statistics(0, 0, 0)

            n_setup = [0]

            def done(ins):
                n_setup[0] += 1
                ins.then_inc(setup_dve, 1)

            ve.wait_ge(setup_pe, 1)
            done(v.tensor_copy(s_wint8, pb[0:SD, 0:D]))
            ve.wait_ge(setup_act, 5)
            done(v.tensor_tensor(wcl[:, :, D:LSC], h1[:, 0:KD * E].rearrange("p (k e) -> p k e", k=KD),
                                 wch[:, :, D:LSC].bitcast(F32), ALU.subtract))
            done(v.tensor_tensor(wgl[:, :, 32:40], s_win[:, :, D:D + SD], wgh[:, :, 32:40].bitcast(F32), ALU.subtract))
            done(v.tensor_tensor(wo[64:64 + SD, :], s_wout8, wo[0:SD, :].bitcast(F32), ALU.subtract))
            statistics(1, 0, 1)
            first_cols = slice(norm_column(0), None)
            variances(2, first_cols)
            scale_and_shift(0, 0, first_cols, s_norm)
            ve.wait_ge(setup_pe, 2)
            done(v.tensor_scalar(gate_bias[:, :], gb[0:SD, 0:1], s_bg, 0.5, ALU.add, ALU.mult))
            ve.wait_ge(setup_act, 8)
            done(v.tensor_tensor(wcl[:, :, 0:D], h3[:, :].rearrange("p (k c) -> p k c", k=KD),
                                 wch[:, :, 0:D].bitcast(F32), ALU.subtract))
            done(v.tensor_tensor(wgl[:, :, 0:SD], yb[:, 0:KD * SD].rearrange("p (k c) -> p k c", k=KD),
                                 wgh[:, :, 0:SD].bitcast(F32), ALU.subtract))
            done(v.tensor_tensor(bias_low.bitcast(F32R), ls[0][0:1, 0:D], wo[96:97, :].bitcast(F32), ALU.subtract))
            assert n_setup[0] == SETUP_DVE

            def split_low(wts, splits, matrices=range(3)):
                for n in matrices:
                    ve.wait_ge(wh_ready, splits + n)
                    v.tensor_tensor(wts[:, 2 * n + 1, :, :], raw_view(n), wts[:, 2 * n, :, :].bitcast(F32),
                                    ALU.subtract).then_inc(wl_ready, 1)

            def statistics_ahead(g, turn, slot):
                ahead = (g + LEAD, turn + (slot + LEAD) // SLOTS, (slot + LEAD) % SLOTS)
                if isinstance(g, int):
                    return
                if slot in (3, 0):
                    with ve.If(turn < GROUPS // SLOTS - (2 if slot else 1)):
                        statistics(*ahead)
                        settled(mean_ready, (g + LEAD + 1) * GT)
                else:
                    statistics(*ahead)
                if slot == 0:
                    variances(g + LEAD - 1)

            def xlow(p, cols, wait=None):
                ve.wait_ge(xh_ready, p + 1)
                if wait is not None:
                    ve.wait_ge(*wait)
                v.tensor_tensor(xl[:, :, cols], xt[:, :].rearrange("p (k t) -> p k t", k=KD),
                                xh[:, :, cols].bitcast(F32), ALU.subtract).then_inc(xl_ready, 1)

            def gate_act(p):
                ve.wait_ge(h3_ready, p + 1)
                ve.wait_ge(silu_ready, p + 1)
                v.tensor_tensor(act[:, :], act[:, :], h3[:, :], ALU.mult).then_inc(act_ready, 1)

            def act_low(p):
                if not is_zero(p):
                    ve.wait_ge(down_ready, p)
                for t in range(2):
                    ve.wait_ge(acth_ready, 2 * p + t + 1)
                    v.tensor_tensor(tile_cols(actl, t), tile_cols(act, t), tile_cols(acth, t).bitcast(F32),
                                    ALU.subtract).then_inc(actl_ready, 1)

            def recurrence(p, i, starts):
                ve.wait_ge(gate_ready, p + 1)
                v.scalar_tensor_tensor(omg, gb[32:32 + SD, 0:PAIR], b_in_state[:, :], omg, ALU.add, ALU.mult
                                       ).then_inc(gated_in, 1)
                if not is_zero(p):
                    ve.wait_ge(states_ready, p)
                    if not is_zero(p - 1):
                        ve.wait_ge(state_high2, p - 1)
                        ve.wait_ge(state_low, p - 1)
                ve.wait_ge(gated_in, p + 1)
                before = GN - 1 if i == 0 else PAIR - 1
                v.tensor_tensor_scan(states[:, region(i)], gate, omg, 0.0 if starts else states[:, before:before + 1],
                                     ALU.mult, ALU.add).then_inc(states_ready, 1)

            def states_low(p, i):
                ve.wait_ge(state_high, p + 1)
                v.tensor_tensor(state_hl[32:32 + SD, region(i)], states[:, region(i)],
                                state_hl[0:SD, region(i)].bitcast(F32), ALU.subtract).then_inc(state_low, 1)

            step = [0]

            def route_link(g, ins):
                step[0] += 1
                ins.then_inc(route_step, 1)
                ve.wait_ge(route_step, g * ROUTE_STEPS + step[0])

            def route_unlinked(g, ins):
                step[0] += 1
                ins.then_inc(route_step, 1)

            def over(ap, shape):
                return ap.to_broadcast(shape)

            def route_centre(g):
                assert step[0] in (0, ROUTE_STEPS), step[0]
                step[0] = 0
                ve.wait_ge(ls_taken, g * GT + GT)
                route_link(g, v.reduce_max(top[:, :], logits[:, :, :], X))
                v.tensor_tensor(ex[:, :, :], logits[:, :, :], over(top[:, :].unsqueeze(2), [P, GT, E]), ALU.subtract
                                ).then_inc(centred, 1)

            def route_groups(g, slot):
                ve.wait_ge(exp_ready, g + 1)
                step[0] += 1
                v.reduce_max(g_max[:, :, 0:EG], ex[:, :, :].rearrange("p t (g e) -> p t g e", g=EG), X
                             ).then_inc(route_step, 1)
                ve.wait_ge(route_step, g * ROUTE_STEPS + step[0])
                v.reduce_sum(total[:, :], ex[:, :, :], X)
                for t in range(GT):
                    v.max(g_top[:, t, 0:8], g_max[:, t, 0:EG]).then_inc(route_step, 1)
                step[0] += GT
                v.tensor_copy(rows[slot][:, :, TOK], token[:, bass.ds(g * GT, GT)])

            def mark_best(g, marked, values, best):
                settled(route_step, g * ROUTE_STEPS + step[0])
                for t in range(GT):
                    v.match_replace(marked[:, t, :], best[:, t, :].rearrange("p (a b) -> p a b", b=4)[:, 0::2, :],
                                    values[:, t, :], MARK).then_inc(route_step, 1)
                step[0] += GT
                ve.wait_ge(route_step, g * ROUTE_STEPS + step[0])

            def route_experts(g):
                mark_best(g, g_marked, g_max, g_top)
                route_link(g, v.tensor_scalar(g_keep[:, :, :], g_marked[:, :, 0:EG], MARK, -4.0, ALU.is_lt, ALU.mult))
                route_unlinked(g, v.tensor_tensor(masked[:, :, 0:E].rearrange("p t (g e) -> p t g e", g=EG),
                                                  ex[:, :, :].rearrange("p t (g e) -> p t g e", g=EG),
                                                  over(g_keep[:, :, :].unsqueeze(3), [P, GT, EG, E // EG]), ALU.add))

            def route_chosen(g):
                settled(route_step, g * ROUTE_STEPS + step[0])
                for t in range(GT):
                    v.max(e_top[:, t, 0:8], masked[:, t, 0:E]).then_inc(route_step, 1)
                step[0] += GT
                mark_best(g, e_marked, masked, e_top)
                v.tensor_scalar(chosen[:, :, :], e_marked[:, :, 0:E], MARK, None, ALU.is_ge).then_inc(chosen_ready, 1)

            def route_weights(g, slot):
                ve.wait_ge(chosen_ready, g + 1)
                route_link(g, v.tensor_tensor(sel[:, :, :], ex[:, :, :], chosen[:, :, :], ALU.mult))
                route_link(g, v.reduce_sum(sel_sum[:, :], sel[:, :, :], X))
                route_link(g, v.scalar_tensor_tensor(sel_sum[:, :], total[:, :], EPS_W, sel_sum[:, :], ALU.mult, ALU.add))
                route_link(g, v.reciprocal(sel_sum[:, :], sel_sum[:, :]))
                v.tensor_tensor(rows[slot][:, :, WCOL:ROW], sel[:, :, :],
                                over(sel_sum[:, :].unsqueeze(2), [P, GT, E]), ALU.mult).then_inc(route_step, 1)
                step[0] += 1

            def route_place(g):
                ve.wait_ge(pos_ready, g + 1)
                route_link(g, v.tensor_tensor(dest[:, :, :], pos, over(row_limit[:, :].unsqueeze(1), [P, GT, E]),
                                              ALU.is_ge))
                v.scalar_tensor_tensor(dest[:, :, :], dest[:, :, :], FAR, pos, ALU.mult, ALU.add).then_inc(pos_taken, 1)
                with nc.allow_low_precision(reason="small whole numbers"):
                    route_unlinked(g, v.reduce_sum(seen_new[:, :], chosen[:, :, :].rearrange("p t e -> p e t"), X))
                ve.wait_ge(pos_taken, g + 1)
                route_unlinked(g, v.scalar_tensor_tensor(dest[:, :, :], dest[:, :, :], 1.0, chosen[:, :, :],
                                                         ALU.add, ALU.mult))

            def route_send(g, slot):
                settled(route_step, g * ROUTE_STEPS + step[0])
                for t in range(GT):
                    v.max(dest_top[:, t, :], dest[:, t, :]).then_inc(route_step, 1)
                step[0] += GT
                ve.wait_ge(route_step, g * ROUTE_STEPS + step[0])
                v.tensor_scalar(dest_idx[slot][:, :, :], dest_top[:, :, 0:K], -1.0, None, ALU.add
                                ).then_inc(dispatch_ready, 1)
                v.tensor_tensor(seen[:, :], seen[:, :], seen_new[:, :], ALU.add).then_inc(seen_ready, 1)
                assert step[0] == ROUTE_STEPS, step[0]

            xlow(0, region(0))
            split_low(w_hl[1], 1)
            statistics(2, 0, 2)
            recurrence(0, 0, True)
            statistics(3, 0, 3)
            states_low(0, 0)

            def group(g, turn, slot):
                before_slot = (slot - 1) % SLOTS
                for i in range(2):
                    p = g * 2 + i
                    has_next = i == 0 or not is_last(g)
                    if i == 0 and slot == 1:
                        scale_and_shift(turn + 1, g + 1)
                    if i == 1 and not is_zero(g):
                        route_weights(g - 1, before_slot)
                    if has_next:
                        xlow(p + 1, region(1 - i), None if is_zero(p) else (h3_ready, p))
                    if is_zero(g):
                        statistics(g + SLOTS + i, 1, i)
                        if i == 1:
                            variances(LEAD + 1)
                    if i == 0:
                        if not is_zero(g):
                            route_groups(g - 1, before_slot)
                            route_experts(g - 1)
                            route_chosen(g - 1)
                    else:
                        if not is_zero(g):
                            route_place(g - 1)
                            route_send(g - 1, before_slot)
                        route_centre(g)
                    if has_next:
                        recurrence(p + 1, 1 - i, i == 1 and slot == SLOTS - 1)
                    gate_act(p)
                    if has_next:
                        states_low(p + 1, 1 - i)
                    if i == 1 and not is_zero(g):
                        statistics_ahead(g, turn, slot)
                    act_low(p)

            group_loop(ve, group)
            last_slot = (GROUPS - 1) % SLOTS
            route_groups(GROUPS - 1, last_slot)
            route_experts(GROUPS - 1)
            route_chosen(GROUPS - 1)
            route_weights(GROUPS - 1, last_slot)
            route_place(GROUPS - 1)
            route_send(GROUPS - 1, last_slot)
            ve.wait_ge(scattered[1], 16 + SCATTERS * (GROUPS // SLOTS))
            v.memset(rows[1][:, 0:2, 0:TOK], 0.0)
            v.memset(rows[1][:, 0:2, WCOL:ROW], 0.0)
            v.memset(rows[1][:, 0:2, TOK:TOK + 1], FAR).then_inc(zero_ready, 1)

            ve.wait_ge(cnt_ready, 1)
            steps = [0]

            def count_link(ins):
                steps[0] += 1
                ins.then_inc(count_step, 1)
                ve.wait_ge(count_step, steps[0])

            count_link(v.tensor_scalar(counts, cnt, float(CAP), None, ALU.min))
            count_link(v.tensor_scalar(n_zeros_f, counts, float(PAIR), 1.0, ALU.is_lt, ALU.add))
            for m in range(2, PAIRS):
                count_link(v.tensor_scalar(n_tmp, counts, float(PAIR * m), None, ALU.is_lt))
                count_link(v.tensor_tensor(n_zeros_f, n_zeros_f, n_tmp, ALU.add))
            count_link(v.tensor_copy(n_rows[:, :], counts[0:1, :]))
            count_link(v.tensor_copy(n_zeros[:, :], n_zeros_f[0:1, :]))
            count_link(v.tensor_scalar(flags_f, counts[0:1, :], float(PAIR * PAIRS), None, ALU.is_gt))
            count_link(v.tensor_copy(has_fifth, flags_f))
            width = 1
            while width < E // 2:
                cols = E - 2 * width + 1
                count_link(v.scalar_tensor_tensor(flags_f[:, 0:cols], flags_f[:, width:width + cols], float(2 ** width),
                                                  flags_f[:, 0:cols], ALU.mult, ALU.add))
                width *= 2
            v.tensor_copy(flags[:, :], flags_f).then_inc(counts_ready, 1)

            split_low(w_hl[0], 4)
            count = PairCounter(ve, "dve")

            def take_meta(q, buf, fills):
                ve.wait_ge(row_loaded[buf], fills * 16)
                v.tensor_copy(meta[:, bass.ds(q % 4, 1), :, :].rearrange("p a t c -> p (a t) c"),
                              row_in[buf][:, :, TOK:ROW]).then_inc(meta_taken, 1)

            def take_y_before(q, e, buf, uses):
                ve.wait_ge(meta_taken, q)
                ve.wait_ge(down_ready, q + A_PAIRS)
                if not is_zero(uses):
                    ve.wait_ge(added[buf], uses)
                for t in range(2):
                    m = meta[:, bass.ds((q + 3) % 4, 1), t, :].rearrange("p a c -> p (a c)")
                    v.tensor_copy(y_idx[:, buf, t:t + 1], m[:, 0:1])
                    v.tensor_scalar(y_out[buf][:, t, :], yb[:, t * D:t * D + D], m[:, bass.ds(e + 1, 1)], None,
                                    ALU.mult).then_inc(y_ready, 1)

            ve.wait_ge(z_stored, 16 * A_PAIRS)
            v.memset(pad[:, :], 0.0).then_inc(y_ready, 2)
            take_meta(0, 1, 1)
            xlow(A_PAIRS, region(0), (h3_ready, A_PAIRS - 1))
            ve.wait_ge(counts_ready, 1)
            count.load_flags()

            def section(e, w_slot, is_first):
                def body(slot):
                    q = count.now()
                    p = q + A_PAIRS
                    fifths = count.fifths_now()
                    take_meta(q + 1, row_buffer(slot), fifths + 1 if slot == PAIRS else row_fills(e, slot))
                    xlow(p + 1, bass.ds(((q + 1) % 2) * PAIR, PAIR), (h3_ready, p))
                    gate_act(p)
                    act_low(p)
                    if not (is_first and slot == 0):
                        take_y_before(q, e - 1 if slot == 0 else e, y_buffer(slot),
                                      fifths * 32 + 16 if slot == PAIRS else y_uses(e, slot) * 32)
                    if slot < 3 and not (isinstance(e, int) and e == E - 1):
                        if slot == 0:
                            ve.wait_ge(down_ready, p)
                        split_low(w_hl[1 - w_slot], e * 3 + 7, (slot,))
                    count.next(slot)
                slots(ve, count, body)

            expert_loop(ve, section)
            take_y_before(count.now(), E - 1, y_buffer(0), y_uses(E, 0) * 32)

            for c in range(CHUNKS):
                ve.wait_ge(silu_y, c + 1)
                v.tensor_tensor(y_buf(c), y_buf(c), s_all[:, tail_tiles(c), :], ALU.mult).then_inc(gated, 1)
                ve.wait_ge(gated, c + 1)
                v.tensor_tensor(y_buf(c), y_buf(c), x_all[:, tail_tiles(c), :], ALU.add).then_inc(out_ready, 1)


SETUP_ACT = 8
SETUP_DVE = 8
DVE_CONSTS = 11

_INS = ["L0_attn_x", "L0_attn_W_in", "L0_attn_b_in", "L0_attn_W_g", "L0_attn_b_g", "L0_attn_W_out", "L0_attn_b_out",
        "L0_ffn_wg", "L0_ffn_w1", "L0_ffn_w2", "L0_ffn_w3", "L0_ffn_sw1", "L0_ffn_sw2", "L0_ffn_sw3"]


def kernel(**inputs):
    import numpy as np
    import concourse.bacc as bacc
    from concourse.bass_utils import run_bass_kernel_spmd

    nc = bacc.Bacc("TRN2", target_bir_lowering=False, num_devices=1)
    arrays, args = {}, []
    for name in _INS:
        a = np.ascontiguousarray(inputs[name])
        arrays[name] = a
        args.append(nc.dram_tensor(name, a.shape, mybir.dt.from_np(a.dtype), kind="ExternalInput").ap())
    out = nc.dram_tensor("out", (B, S, D), F32, kind="ExternalOutput").ap()
    build(nc, *args, out)
    r = run_bass_kernel_spmd(nc, [arrays], core_ids=[0])
    return r.results[0]["out"]
```
